# Optimizing a Trainium2 kernel written in Bass

```python
import numpy as np
import jax
import jax.numpy as jnp

def _softmax(x, axis=-1):
    return jax.nn.softmax(x, axis=axis)

def _gelu(x):
    return jax.nn.gelu(x, approximate=True)

def _silu(x):
    return jax.nn.silu(x)

def _sigmoid(x):
    return jax.nn.sigmoid(x)

def _layernorm(x, axis=-1, eps=1e-05):
    m = jnp.mean(x, axis=axis, keepdims=True)
    v = jnp.var(x, axis=axis, keepdims=True)
    return (x - m) / jnp.sqrt(v + eps)

def _scatter_add(tgt, idx, src, axis=0):
    return tgt.at[idx].add(src)

def _segment_sum(src, seg, n):
    return jax.ops.segment_sum(src, seg, n)
kernel_name = 'mk_flamingo_gated_d1_seqx_r4_4439c9'

def setup_inputs(seed: int=0):
    np.random.seed(seed)
    _w = jnp.asarray

    def _rec_inputs():
        import jax
        import jax.numpy as jnp
        _rk = jax.random.key(seed)
        x = -7.109e-05 + 0.9999 * jax.random.normal(jax.random.fold_in(_rk, 1), (4, 512, 512), jnp.float32)
        _lenS = 512 - jax.random.randint(jax.random.fold_in(_rk, 7), (4,), 0, max(1, 512 // 4) + 1, jnp.int32)
        _lenS2 = 512 - jax.random.randint(jax.random.fold_in(_rk, 8), (4,), 0, max(1, 512 // 4) + 1, jnp.int32)
        _ctx_2048P = jax.random.normal(jax.random.fold_in(_rk, 11), (4, 16, 512), jnp.float32)
        _ctx_2048c = jax.random.dirichlet(jax.random.fold_in(_rk, 511), 0.3 * jnp.ones((16,), jnp.float32), (4, 512))
        _ctx_2048t = jnp.einsum('bsk,bkd->bsd', _ctx_2048c, _ctx_2048P)
        _ctx_2048t = _ctx_2048t * jax.lax.rsqrt(jnp.mean(jnp.square(_ctx_2048t)) + 1e-12) * 0.953939
        ctx_2048 = -3.05549e-07 + 0.0199987 * (_ctx_2048t + 0.3 * jax.random.normal(jax.random.fold_in(_rk, 611), (4, 512, 512), jnp.float32))
        _g = jax.random.normal(jax.random.fold_in(_rk, 9001), (2, 1), jnp.float32)
        _g = jnp.sign(_g) * jnp.maximum(jnp.abs(_g), 1.0) + (_g == 0) * 1.0
        g_xattn = _g[0]
        g_ffn = _g[1]
        return (x, ctx_2048, g_xattn, g_ffn)
    x, ctx_2048, g_xattn, g_ffn = _rec_inputs()

    def _L0_xattn_setup():
        import jax, jax.numpy as jnp
        import numpy as np
        FP8_MAX = 448.0
        ACT_EPS = 0.0001
        W_EPS = 1e-06
        BLK = 128

        def quant_dequant_act_1x128(x):
            E, M, K = x.shape
            xb = x.reshape(E, M, K // BLK, BLK)
            amax = jnp.max(jnp.abs(xb), axis=-1, keepdims=True)
            safe = jnp.maximum(amax, ACT_EPS)
            q = (xb * (FP8_MAX / safe)).astype(jnp.float8_e4m3fn)
            return (q.astype(jnp.float32) * (safe / FP8_MAX)).reshape(E, M, K)

        def quant_dequant_weight_128x128(w):
            E, N, K = w.shape
            wb = w.reshape(E, N // BLK, BLK, K // BLK, BLK)
            amax = jnp.max(jnp.abs(wb), axis=(2, 4), keepdims=True)
            safe = jnp.maximum(amax, W_EPS)
            q = (wb * (FP8_MAX / safe)).astype(jnp.float8_e4m3fn)
            return (q.astype(jnp.float32) * (safe / FP8_MAX)).reshape(E, N, K)
        key = jax.random.key(seed)
        kx, kw = jax.random.split(key)
        E, M, K, N = (8, 1024, 512, 512)
        x = jax.random.normal(kx, (E, M, K), dtype=jnp.float32)
        weight = jax.random.normal(kw, (E, N, K), dtype=jnp.float32) * 0.02
        return {'x': x, 'weight': weight}
    _L0_xattn_all = _L0_xattn_setup()
    _L0_xattn_in = {k: v for k, v in _L0_xattn_all.items() if k in ()}
    del _L0_xattn_all

    def _L0_ffn_setup():
        import jax, jax.numpy as jnp
        import numpy as np
        N_HEAD = 16
        N_EMBD = 512
        R = 8
        HEAD_DIM = N_EMBD // N_HEAD
        D_STD = HEAD_DIM - R
        THRESHOLD = 0.1
        B, T = (4, 256)
        key = jax.random.key(seed)
        k1, k2, k3, k4, k5 = jax.random.split(key, 5)
        fused_dim = 2 * N_HEAD * D_STD + N_EMBD + 2 * N_HEAD * R
        x = jax.random.normal(k1, (B, T, N_EMBD), dtype=jnp.float32)
        Wa = jax.random.normal(k2, (N_EMBD, fused_dim), dtype=jnp.float32) * 0.02
        Wp = jax.random.normal(k3, (N_EMBD, N_EMBD), dtype=jnp.float32) * 0.02
        w_std = jax.random.uniform(k4, (N_HEAD,), dtype=jnp.float32, minval=0.3, maxval=0.7)
        w_rec = jax.random.uniform(k5, (N_HEAD,), dtype=jnp.float32)
        return {'x': x, 'Wa': Wa, 'Wp': Wp, 'w_std': w_std, 'w_rec': w_rec}
    _L0_ffn_all = _L0_ffn_setup()
    _L0_ffn_in = {k: v for k, v in _L0_ffn_all.items() if k in ('Wa', 'Wp', 'w_std', 'w_rec')}
    del _L0_ffn_all
    return {'x': x, 'ctx_2048': ctx_2048, 'g_xattn': g_xattn, 'g_ffn': g_ffn, 'L0_ffn_Wa': _L0_ffn_in['Wa'], 'L0_ffn_Wp': _L0_ffn_in['Wp'], 'L0_ffn_w_std': _L0_ffn_in['w_std'], 'L0_ffn_w_rec': _L0_ffn_in['w_rec']}

def reference(x, ctx_2048, g_xattn, g_ffn, L0_ffn_Wa, L0_ffn_Wp, L0_ffn_w_std, L0_ffn_w_rec):
    import jax
    import jax.numpy as jnp

    def _L0_xattn_ref(x, weight):
        import jax, jax.numpy as jnp
        import numpy as np
        FP8_MAX = 448.0
        ACT_EPS = 0.0001
        W_EPS = 1e-06
        BLK = 128

        def quant_dequant_act_1x128(x):
            E, M, K = x.shape
            xb = x.reshape(E, M, K // BLK, BLK)
            amax = jnp.max(jnp.abs(xb), axis=-1, keepdims=True)
            safe = jnp.maximum(amax, ACT_EPS)
            q = (xb * (FP8_MAX / safe)).astype(jnp.float8_e4m3fn)
            return (q.astype(jnp.float32) * (safe / FP8_MAX)).reshape(E, M, K)

        def quant_dequant_weight_128x128(w):
            E, N, K = w.shape
            wb = w.reshape(E, N // BLK, BLK, K // BLK, BLK)
            amax = jnp.max(jnp.abs(wb), axis=(2, 4), keepdims=True)
            safe = jnp.maximum(amax, W_EPS)
            q = (wb * (FP8_MAX / safe)).astype(jnp.float8_e4m3fn)
            return (q.astype(jnp.float32) * (safe / FP8_MAX)).reshape(E, N, K)
        xq = quant_dequant_act_1x128(x)
        wq = quant_dequant_weight_128x128(weight)
        return jnp.einsum('emk,enk->emn', xq, wq)

    def _L0_ffn_ref(x, Wa, Wp, w_std, w_rec):
        import jax, jax.numpy as jnp
        import numpy as np
        N_HEAD = 16
        N_EMBD = 512
        R = 8
        HEAD_DIM = N_EMBD // N_HEAD
        D_STD = HEAD_DIM - R
        THRESHOLD = 0.1
        B, T = (4, 256)
        Bx, Tx, C = x.shape
        H, D, Ds, r = (N_HEAD, HEAD_DIM, D_STD, R)
        s_std = jnp.sqrt(jnp.clip(w_std, 1e-08, None))
        s_rec = jnp.sqrt(jnp.clip(w_rec, 1e-08, None))
        col_scale = jnp.concatenate([jnp.repeat(s_std, Ds), jnp.repeat(s_std, Ds), jnp.ones((C,), dtype=x.dtype), jnp.repeat(s_rec, r), jnp.repeat(s_rec, r)])
        Wb = Wa * col_scale[None, :]
        fused = x @ Wb
        q_std_end = H * Ds
        k_std_end = q_std_end + H * Ds
        v_end = k_std_end + C
        q_low_end = v_end + H * r

        def heads(t, d):
            return t.reshape(Bx, Tx, H, d).transpose(0, 2, 1, 3)
        Q_std = heads(fused[..., :q_std_end], Ds)
        K_std = heads(fused[..., q_std_end:k_std_end], Ds)
        V = heads(fused[..., k_std_end:v_end], D)
        Q_low = heads(fused[..., v_end:q_low_end], r)
        K_low = heads(fused[..., q_low_end:], r)
        use_ra = (w_rec > THRESHOLD)[None, :, None, None]
        q_tail = jnp.where(use_ra, K_low, Q_low)
        k_tail = jnp.where(use_ra, Q_low, K_low)
        Qf = jnp.concatenate([Q_std, q_tail], axis=-1)
        Kf = jnp.concatenate([K_std, k_tail], axis=-1)
        scale = 1.0 / jnp.sqrt(jnp.asarray(D, dtype=x.dtype))
        scores = jnp.einsum('bhtd,bhsd->bhts', Qf, Kf) * scale
        causal = jnp.tril(jnp.ones((Tx, Tx), dtype=bool))
        scores = jnp.where(causal[None, None], scores, jnp.finfo(scores.dtype).min)
        attn = jax.nn.softmax(scores, axis=-1)
        out = jnp.einsum('bhts,bhsd->bhtd', attn, V)
        y = out.transpose(0, 2, 1, 3).reshape(Bx, Tx, C)
        return y @ Wp
    x = x + jnp.tanh(g_xattn[0]) * _L0_xattn_ref(_layernorm(x, axis=-1), ctx_2048)
    x = x + jnp.tanh(g_ffn[0]) * _L0_ffn_ref(_layernorm(x, axis=-1), L0_ffn_Wa, L0_ffn_Wp, L0_ffn_w_std, L0_ffn_w_rec)
    return x

_drawn_inputs = setup_inputs


def setup_inputs(seed=0):
    import zlib

    import numpy as np

    out = dict(_drawn_inputs(seed))
    spreads = {}
    factors = {'L0_ffn_Wa': 2.674, 'L0_ffn_Wp': 2.699, 'L0_ffn_w_std': 8.0, 'L0_ffn_w_rec': 8.0}
    for name, (base, spread) in spreads.items():
        noise = np.random.default_rng([zlib.crc32(name.encode()), seed]).standard_normal(out[name].shape)
        drawn = base * np.exp(spread * noise) if base else spread * noise
        out[name] = jnp.asarray(drawn.astype(out[name].dtype))
    for name, factor in factors.items():
        out[name] = (out[name] * factor).astype(out[name].dtype)
    return out
```

```python
import concourse.bass as bass
from concourse import mybir
from concourse.alu_op_type import AluOpType as ALU
from contextlib import ExitStack

FP32 = mybir.dt.float32
FP32R = mybir.dt.float32r
BF16 = mybir.dt.bfloat16
U16 = mybir.dt.uint16
U32 = mybir.dt.uint32
ACT = mybir.ActivationFunctionType
AX = mybir.AxisListType

B, T, C = 4, 512, 512
H, D, R = 16, 32, 8
DS = D - R
P = 128
NT = T // P
NK = C // P
NF = 3 * C
STEPS = H // 2
SLOTS = 4
SCALE = float(D) ** -0.5
FP8_MAX, ACT_EPS, W_EPS, LN_EPS = 448.0, 1e-4, 1e-6, 1e-5
MAGIC, MIN_NORMAL, EXPONENT_BITS = 1.5 * 2.0 ** 20, 2.0 ** -6, 0x7F80

MAX_UNITS = [[(3, 0)], [(2, 0), (0, 384)], [(1, 0)]]
EXP_UNITS = [[(0, 0)], [(1, 0), (3, 384)], [(2, 0)]]
PROB_COL = [0, 512, 1024, 896]
UNIT_COL = [0, 512, 1024]
UNIT_LEN = [512, 512, 256]

FILL = [
    ["V0 V1", "V2 V3", "", ""],
    ["Q2", "K2", "W0", "W1"],
    ["Q3", "K3", "W2", "W3"],
    ["X0", "", "X1", "X2"],
    ["X3", "S0", "S1", ""],
    ["S2", "S3", "H0", "H1"],
    ["H2", "H3", "q0", "k0"],
    ["q1", "k1", "", ""],
]
DVE_CHAIN, POOL_CHAIN = 43, 19


def pieces(gap, more):
    for name in gap.split():
        if more or name[0] in "VQK":
            yield name[0], int(name[1])


class Chain:

    def __init__(self, eng, sem):
        self.eng, self.sem, self.base, self.n = eng, sem, 0, 0

    def __call__(self, ins, wait=lambda eng, sem, count: eng.wait_ge(sem, count)):
        self.n += 1
        ins.then_inc(self.sem, 1)
        wait(self.eng, self.sem, self.base + self.n)

    def at(self, base):
        self.base, self.n = base, 0


def flamingo_block(nc, x, ctx, g_xattn, g_ffn, wa, wp, w_std, w_rec, out):
    es = ExitStack()
    with es:
        def sb(name, shape, dt=FP32):
            return es.enter_context(nc.sbuf_tensor(name, shape, dt))

        def pb(name, dt=FP32):
            return es.enter_context(nc.psum_tensor(name, [P, 512], dt))

        def sem(name):
            return es.enter_context(nc.semaphore(name))

        w_hi, w_lo = sb("w_hi", [P, NK, NF], FP32R), sb("w_lo", [P, NK, NF], FP32R)
        wp_hi, wp_lo = sb("wp_hi", [P, NK, C], FP32R), sb("wp_lo", [P, NK, C], FP32R)
        q_stack = sb("q_stack", [97, SLOTS, 2, T], FP32R)
        k_stack = sb("k_stack", [97, SLOTS, 2, T], FP32R)
        qk_hi = sb("qk_hi", [P, 2, 2, T], FP32R)
        qk_lo = sb("qk_lo", [P, 2, 2, T], FP32R)
        xt_hi, xt_lo = sb("xt_hi", [P, NK, T], FP32R), sb("xt_lo", [P, NK, T], FP32R)
        wt_hi, wt_lo = sb("wt_hi", [P, NK, T], FP32R), sb("wt_lo", [P, NK, T], FP32R)
        x_all = sb("x_all", [P, 2, NT, C])
        ctx_raw = sb("ctx_raw", [P, NT, C])
        tile_buf = sb("tile_buf", [P, 4, C])
        magic = sb("magic", [P, 2, C], BF16)
        v_aug = sb("v_aug", [P, NT, H, D + 1])
        work = sb("work", [P, 4608])
        prob = [work[:, 0:1280], work[:, 1280:2560]]
        y = work[:, 2560:4608].rearrange("p (i c) -> p i c", i=NT)
        ident = sb("ident", [P, P])
        ident_bf = sb("ident_bf", [P, P], BF16)
        future = sb("future", [P, P], BF16)
        gates = sb("gates", [P, 2])
        wsr = sb("wsr", [P, 2, H])
        wsr_root = sb("wsr_root", [P, 2, H])
        neg_half = sb("neg_half", [P, NT])
        spare = x_all[:, 1, 0, :]
        tails = spare[:, 0:2 * H * R].rearrange("p (q h e) -> p q h e", q=2, h=H)
        swap = spare[:, 256:256 + H * R].bitcast(U32).rearrange("p (h e) -> p h e", h=H)
        half = spare[:, 384:384 + 2 * H].rearrange("p (q h) -> p q h", q=2)
        w_amax, w_top = sb("w_amax", [P, NT * NK]), sb("w_top", [P, NT * NK])
        w_up, w_down = sb("w_up", [P, NT * NK]), sb("w_down", [P, NT * NK])
        x_amax = sb("x_amax", [P, NT, NK])
        x_up, x_down = sb("x_up", [P, NT, NK]), sb("x_down", [P, NT, NK])
        bn1, mv1 = sb("bn1", [P, NT, 6]), sb("mv1", [P, NT, 2])
        bn2, mv2 = sb("bn2", [P, NT, 6]), sb("mv2", [P, NT, 2])
        rstd1, rstd2 = sb("rstd1", [P, NT]), sb("rstd2", [P, NT])
        row_max = sb("row_max", [P, 8])
        neg_max = sb("neg_max", [8, P], FP32R)
        rden = sb("rden", [P, 8])

        max_bank = [pb("max_bank0"), pb("max_bank1")]
        exp_bank = [pb("exp_bank0"), pb("exp_bank1")]
        pv_bank = pb("pv_bank")
        turn_bank = pb("turn_bank")
        mm_bank = [pb("mm_bank0"), pb("mm_bank1")]

        s_begun = sem("s_begun")
        s_const = sem("s_const")
        s_small = sem("s_small")
        s_tanh = sem("s_tanh")
        s_root = sem("s_root")
        s_wload = [sem(f"s_wload{i}") for i in range(NK + 1)]
        s_wscaled = sem("s_wscaled")
        s_whi = sem("s_whi")
        s_wlo = sem("s_wlo")
        s_xload = [sem(f"s_xload{i}") for i in range(NT)]
        s_ctxload = [sem(f"s_ctxload{i}") for i in range(NT)]
        s_amax = sem("s_amax")
        s_top = sem("s_top")
        s_wscale = sem("s_wscale")
        s_var1, s_rstd1 = sem("s_var1"), sem("s_rstd1")
        s_rstd2 = sem("s_rstd2")
        s_xscale = sem("s_xscale")
        s_scaled = sem("s_scaled")
        s_magic = sem("s_magic")
        s_quant = sem("s_quant")
        s_hn = sem("s_hn")
        s_turn = sem("s_turn")
        s_thi, s_tlo = sem("s_thi"), sem("s_tlo")
        s_cross, s_x1 = sem("s_cross"), sem("s_x1")
        s_qk, s_qkhi, s_qklo = sem("s_qk"), sem("s_qkhi"), sem("s_qklo")
        s_v, s_vcopy = sem("s_v"), sem("s_vcopy")
        s_stack = [sem(f"s_stack{i}") for i in range(SLOTS)]
        s_negrow = [sem(f"s_negrow{i}") for i in range(SLOTS)]
        s_sm, s_max = sem("s_sm"), sem("s_max")
        s_mt, s_neg = sem("s_mt"), sem("s_neg")
        s_st, s_exp = sem("s_st"), sem("s_exp")
        s_causal = sem("s_causal")
        s_pv, s_norm = sem("s_pv"), sem("s_norm")
        s_yt, s_yhi, s_ylo = sem("s_yt"), sem("s_yhi"), sem("s_ylo")
        s_wpmm = sem("s_wpmm")
        s_outt = sem("s_outt")
        s_store = sem("s_store")
        s_dve = sem("s_dve")
        s_pool = sem("s_pool")

        FIRST_OUT = NT

        def wait_apart(eng, sem, count):
            if not isinstance(count, int):
                count = eng.to_reg(count)
                eng.wait_ge(s_begun, 1)
            eng.wait_ge(sem, count)

        def per_batch(eng, body):
            with eng.Fori(0, B - 1) as b:
                body(b, True)
            body(B - 1, False)

        block = es.enter_context(nc.Block())

        @block.sync
        def _(sp):
            x_v = x.rearrange("b (i p) c -> b i p c", p=P)
            ctx_v = ctx.rearrange("b (i p) c -> b i p c", p=P)
            out_v = out.rearrange("b (i p) c -> b i p c", p=P)

            def load_tiles(n, parity):
                for i in range(NT):
                    sp.dma_start(x_all[:, parity, i, :], x_v[n, i, :, :]).then_inc(s_xload[i], 16)
                for i in range(NT):
                    sp.dma_start(ctx_raw[:, i, :], ctx_v[n, i, :, :]).then_inc(s_ctxload[i], 16)

            def stack(n, u, first=False):
                g, s = u // 2, u % SLOTS
                wait_apart(sp, s_qklo, 8 * n + 2 * g + 2)
                if not first:
                    wait_apart(sp, s_st, 48 * n + 6 * (u - SLOTS) + 6)
                for j in range(2):
                    rows = slice(D * (2 * (u % 2) + j), D * (2 * (u % 2) + j) + D)
                    for dst, w, parts in ((q_stack, 0, (qk_hi, qk_lo, qk_hi)),
                                          (k_stack, 1, (qk_hi, qk_hi, qk_lo))):
                        for a, part in enumerate(parts):
                            sp.dma_start(dst[D * a:D * a + D, s, j, :].bitcast(FP32),
                                         part[rows, g % 2, w, :].bitcast(FP32)).then_inc(s_stack[s], 16)

            load_tiles(0, 0)
            wa_v = wa.rearrange("(k p) f -> p k f", p=P)
            for k in range(NK):
                if k == NK - 1:
                    sp.wait_ge(s_wlo, 1)
                sp.dma_start(work[:, NF * (k % 3):NF * (k % 3) + NF], wa_v[:, k, :]).then_inc(s_wload[k], 16)
            sp.wait_ge(s_wlo, 3)
            sp.dma_start(work[:, NF:NF + NK * C].rearrange("p (k c) -> p k c", k=NK),
                         wp.rearrange("(k p) c -> p k c", p=P)).then_inc(s_wload[NK], 16)
            for u in range(SLOTS):
                stack(0, u, first=True)

            def body(b, more):
                if more:
                    wait_apart(sp, s_scaled, 8 * b + 8)
                    for i in range(NT):
                        sp.dma_start(x_all[:, bass.ds((b + 1) % 2, 1), i, :], x_v[bass.ds(b + 1, 1), i, :, :]
                                     .rearrange("a p c -> p a c")).then_inc(s_xload[i], 16)
                    for i in range(NT):
                        sp.dma_start(ctx_raw[:, i:i + 1, :], ctx_v[bass.ds(b + 1, 1), i, :, :]
                                     .rearrange("a p c -> p a c")).then_inc(s_ctxload[i], 16)
                for u in range(SLOTS, STEPS):
                    stack(b, u)
                if more:
                    for u in range(SLOTS):
                        stack(b + 1, u)
                for i in range(NT):
                    wait_apart(sp, s_outt, FIRST_OUT + NT * b + i + 1)
                    if more:
                        sp.dma_start(out_v[bass.ds(b, 1), i, :, :].rearrange("a p c -> p a c"),
                                     x_all[:, bass.ds(b % 2, 1), i, :]).then_inc(s_store, 16)
                    else:
                        sp.dma_start(out_v[b, i, :, :], x_all[:, b % 2, i, :]).then_inc(s_store, 16)
                wait_apart(sp, s_store, 16 * NT * b + 16 * NT)

            per_batch(sp, body)

        @block.gpsimd
        def _(pool):
            chain = Chain(pool, s_pool)
            pool.memset(neg_half[:], -0.5).then_inc(s_begun, 1)
            chain(pool.memset(ident[:], 0.0))
            chain(pool.affine_select(out=ident[:], in_=ident[:], compare_op=ALU.not_equal, fill=1.0,
                                     base=0, pattern=[[-1, P]], channel_multiplier=1))
            pool.tensor_copy(ident_bf[:], ident[:]).then_inc(s_const, 1)
            chain(pool.memset(future[:], 0.0))
            pool.affine_select(out=future[:], in_=future[:], compare_op=ALU.is_ge, fill=-3.0e38,
                               base=0, pattern=[[-1, P]], channel_multiplier=1).then_inc(s_const, 1)
            pool.wait_ge(s_const, 2)
            pool.memset(k_stack[96:97, :, :, :].bitcast(FP32), 1.0).then_inc(s_const, 1)
            pool.wait_ge(s_const, 3)
            chain(pool.memset(half, 0.5))
            pool.wait_ge(s_small, 64)
            chain(pool.tensor_scalar(wsr_root[:], wsr[:], 1e-8, None, ALU.max))
            chain(pool.tensor_tensor(wsr_root[:], wsr_root[:], half, ALU.pow))
            pool.memset(v_aug[:, :, :, D:D + 1], 1.0).then_inc(s_root, 1)

            def top(n):
                wait_apart(pool, s_amax, n + 1)
                pool.partition_all_reduce(w_top[:], w_amax[:], P, bass.bass_isa.ReduceOp.max).then_inc(s_top, 1)

            def inv_std(n, mv, rstd, lo, hi, var_sem, rstd_sem, count):
                wait_apart(pool, var_sem, count)
                chain(pool.tensor_scalar(rstd[:, lo:hi], mv[:, lo:hi, 1], LN_EPS, None, ALU.add))
                pool.tensor_tensor(rstd[:, lo:hi], rstd[:, lo:hi], neg_half[:, lo:hi], ALU.pow).then_inc(rstd_sem, 1)

            def inv_std1(n):
                inv_std(n, mv1, rstd1, 0, NT, s_var1, s_rstd1, n + 1)

            def inv_std2(n, pair):
                inv_std(n, mv2, rstd2, 2 * pair, 2 * pair + 2, s_x1, s_rstd2, NT * n + 2 * pair + 2)

            def blocks(ap):
                return ap.rearrange("p (k c) -> p k c", k=NK)

            def spread(scales):
                return scales.unsqueeze(2).broadcast_to([P, NK, P])

            def scale_up(n, k):
                buf = tile_buf[:, k % 4, :]
                if k < NT:
                    if k == 0:
                        pool.wait_ge(s_wscale, n + 1)
                    src, up = ctx_raw[:, k, :], w_up[:, NK * k:NK * k + NK]
                else:
                    pool.wait_ge(s_xscale, NT * n + k - NT + 1)
                    src, up = buf, x_up[:, k - NT, :]
                pool.tensor_tensor(blocks(buf), blocks(src), spread(up), ALU.mult).then_inc(s_scaled, 1)

            def quantise(n, k):
                buf = tile_buf[:, k % 4, :]
                down = w_down[:, NK * k:NK * k + NK] if k < NT else x_down[:, k - NT, :]
                pool.wait_ge(s_magic, 8 * n + k + 1)
                chain(pool.tensor_tensor(buf, buf, magic[:, k % 2, :], ALU.add))
                chain(pool.tensor_tensor(buf, buf, magic[:, k % 2, :], ALU.subtract))
                pool.tensor_tensor(blocks(buf), blocks(buf), spread(down), ALU.mult).then_inc(s_quant, 1)

            def zero_future(b, u, j):
                wait_apart(pool, s_exp, 48 * b + 6 * u + 3 * j + 3)
                three = prob[j].rearrange("p (a c) -> p a c", c=256)[:, 0:5:2, 0:P]
                pool.affine_select(out=three, in_=three, compare_op=ALU.is_ge, fill=0.0,
                                   base=0, pattern=[[0, 3], [1, P]], channel_multiplier=-1)
                last = prob[j][:, PROB_COL[3]:PROB_COL[3] + P]
                pool.affine_select(out=last, in_=last, compare_op=ALU.is_ge, fill=0.0,
                                   base=0, pattern=[[1, P]], channel_multiplier=-1).then_inc(s_causal, 1)

            top(0)
            inv_std1(0)
            scale_up(0, 0)
            scale_up(0, 1)
            for k in range(8):
                quantise(0, k)
                if k + 2 < 8:
                    scale_up(0, k + 2)
            inv_std2(0, 0)
            inv_std2(0, 1)
            first = chain.n

            def body(b, more):
                n = b + 1
                chain.at(first + POOL_CHAIN * b)
                gaps = {0: [[(top, ()), (inv_std1, ())], [(scale_up, (0,))], [(scale_up, (1,)), (quantise, (0,))]],
                        1: [[(scale_up, (2,))], [(quantise, (1,))], [(scale_up, (3,)), (quantise, (2,))]],
                        2: [[(scale_up, (4,))], [(quantise, (3,))], [(scale_up, (5,)), (quantise, (4,))]],
                        3: [[], [(scale_up, (6,)), (quantise, (5,))], [(scale_up, (7,)), (quantise, (6,))]],
                        4: [[(quantise, (7,))], [], [(inv_std2, (0,))]],
                        5: [[], [(inv_std2, (1,))], []]}
                for u in range(STEPS):
                    before, between, after = gaps.get(u, [[], [], []]) if more else [[], [], []]
                    for f, a in before:
                        f(n, *a)
                    zero_future(b, u, 0)
                    for f, a in between:
                        f(n, *a)
                    zero_future(b, u, 1)
                    for f, a in after:
                        f(n, *a)
                if more:
                    assert chain.n == POOL_CHAIN, chain.n

            per_batch(pool, body)

        @block.tensor
        def _(pe):
            def split_product(dst, l_hi, l_lo, r_hi, r_lo, done):
                for k in range(NK):
                    pe.matmul(dst, l_hi(k), r_hi(k), start=(k == 0), stop=False)
                    pe.matmul(dst, l_hi(k), r_lo(k), start=False, stop=False)
                    last = pe.matmul(dst, l_lo(k), r_hi(k), start=False, stop=(k == NK - 1))
                last.then_inc(done, 1)

            def turn(src, done):
                for k in range(NK):
                    last = pe.transpose(turn_bank[:, P * k:P * k + P], src[:, P * k:P * k + P], ident[:])
                last.then_inc(done, 1)

            def rows_of(t, i):
                return lambda k: t[:, k, P * i:P * i + P]

            def cols_of(t, lo, n):
                return lambda k: t[:, k, lo:lo + n]

            def side(kind, i, n, more, first=False):
                if kind in "WX":
                    k = i + (NT if kind == "X" else 0)
                    pe.wait_ge(s_quant, 8 * n + k + 1)
                    if k:
                        pe.wait_ge(s_tlo, 12 * n + k)
                    turn(tile_buf[:, k % 4, :], s_turn)
                elif kind == "H":
                    pe.wait_ge(s_hn, NT * n + i + 1)
                    pe.wait_ge(s_tlo, 12 * n + 8 + i)
                    turn(tile_buf[:, i % 4, :], s_turn)
                elif kind == "S":
                    if i >= 2:
                        pe.wait_ge(s_x1, NT * n + i - 1)
                    elif not first:
                        pe.wait_ge(s_qklo, 8 * n - 1 + i)
                    pe.wait_ge(s_tlo, 12 * n + NT + i + 1)
                    split_product(mm_bank[i % 2][:], rows_of(xt_hi, i), rows_of(xt_lo, i),
                                  cols_of(wt_hi, 0, C), cols_of(wt_lo, 0, C), s_cross)
                elif kind == "V":
                    if i < 2:
                        pe.wait_ge(s_outt, FIRST_OUT + NT * n - 1 + i)
                        pe.wait_ge(s_qklo, 8 * n + 3 + i)
                    else:
                        pe.wait_ge(s_vcopy, NT * n + i - 1)
                    split_product(mm_bank[i % 2][:], rows_of(xt_hi, i), rows_of(xt_lo, i),
                                  cols_of(w_hi, 2 * C, C), cols_of(w_lo, 2 * C, C), s_v)
                else:
                    w, g = (0 if kind in "qQ" else 1), i
                    if g == 0:
                        pe.wait_ge(s_x1, NT * n + 3 + w)
                    elif g == 2:
                        pe.wait_ge(s_vcopy, NT * n + 3 + w)
                    else:
                        pe.wait_ge(s_qklo, 8 * n + 2 * g - 1 + w)
                    if g == 0:
                        pe.wait_ge(s_tlo, 12 * n + 12)
                    at = C * w + P * g
                    split_product(mm_bank[w][:], cols_of(w_hi, at, P), cols_of(w_lo, at, P),
                                  cols_of(xt_hi, 0, T), cols_of(xt_lo, 0, T), s_qk)

            def scores_for_max(n, u, j, k, first=False):
                s, unit = u % SLOTS, 3 * j + k
                if unit == 0:
                    pe.wait_ge(s_stack[s], 192 * (2 * n + u // SLOTS + 1))
                    if not first:
                        pe.wait_ge(s_neg, 8 * n + u)
                if unit >= 2 or not first:
                    pe.wait_ge(s_max, 48 * n + 6 * u + unit - 1)
                bank = max_bank[unit % 2]
                for i, col in MAX_UNITS[k]:
                    width = P * (i + 1)
                    pe.matmul(bank[:, col:col + width], q_stack[0:96, s, j, P * i:P * i + P],
                              k_stack[0:96, s, j, 0:width], start=True, stop=False)
                    last = pe.matmul(bank[:, col + P * i:col + width], ident_bf[:], future[:],
                                     start=False, stop=True)
                last.then_inc(s_sm, 1)

            def transpose_max(n, u):
                pe.wait_ge(s_max, 48 * n + 6 * u + 6)
                pe.transpose(max_bank[0][0:8, 0:P], row_max[:], ident[:]).then_inc(s_mt, 1)

            def scores_t(b, u, j, k):
                s, unit = u % SLOTS, 3 * j + k
                if unit == 0:
                    pe.wait_ge(s_negrow[s], 16 * (2 * b + u // SLOTS + 1))
                if unit >= 2:
                    pe.wait_ge(s_exp, 48 * b + 6 * u + unit - 1)
                bank = exp_bank[unit % 2]
                for i, col in EXP_UNITS[k]:
                    last = pe.matmul(bank[:, col:col + T - P * i], k_stack[0:97, s, j, P * i:P * i + P],
                                     q_stack[0:97, s, j, P * i:T], start=True, stop=True)
                last.then_inc(s_st, 1)

            def weighted_values(b, u, j):
                if u == 0 and j == 0:
                    pe.wait_ge(s_vcopy, NT * b + NT)
                if u and j == 0:
                    pe.wait_ge(s_norm, 8 * b + u)
                pe.wait_ge(s_causal, 16 * b + 2 * u + j + 1)
                for i in range(NT):
                    dst = pv_bank[:, (NT * j + i) * (D + 1):(NT * j + i + 1) * (D + 1)]
                    for m in range(i + 1):
                        at = PROB_COL[m] + P * (i - m)
                        last = pe.matmul(dst, prob[j][:, at:at + P], v_aug[:, m, 2 * u + j, :],
                                         start=(m == 0), stop=(m == i))
                last.then_inc(s_pv, 1)

            def turn_y(b, i):
                if i == 0:
                    pe.wait_ge(s_norm, 8 * b + 8)
                else:
                    pe.wait_ge(s_ylo, NT * b + i)
                turn(y[:, i, :], s_yt)

            def out_product(b, i, more):
                if i < 2:
                    pe.wait_ge(s_qklo, 8 * b + (11 if more else 7) + i)
                else:
                    pe.wait_ge(s_outt, FIRST_OUT + NT * b + i - 1)
                pe.wait_ge(s_ylo, NT * b + i + 1)
                split_product(mm_bank[i % 2][:], rows_of(wt_hi, i), rows_of(wt_lo, i),
                              cols_of(wp_hi, 0, C), cols_of(wp_lo, 0, C), s_wpmm)

            pe.wait_ge(s_const, 1)
            for name in "W0 W1 W2 W3 X0 X1 X2 X3 S0 S1 S2 S3 H0 H1 H2 H3".split():
                side(name[0], int(name[1]), 0, True, first=True)
            pe.wait_ge(s_wlo, NK + 1)
            for g in range(2):
                side("q", g, 0, True)
                side("k", g, 0, True)
            pe.wait_ge(s_const, 3)
            for unit in range(6):
                scores_for_max(0, 0, unit // 3, unit % 3, first=True)
            transpose_max(0, 0)

            def body(b, more):
                def fill(u, gap):
                    for kind, i in pieces(FILL[u][gap], more):
                        side(kind, i, b if kind in "VQK" else b + 1, more)

                for u in range(STEPS):
                    ahead = u + 1 < STEPS
                    if ahead:
                        scores_for_max(b, u + 1, 0, 0)
                        scores_for_max(b, u + 1, 0, 1)
                    fill(u, 0)
                    scores_t(b, u, 0, 0)
                    scores_t(b, u, 0, 1)
                    if ahead:
                        scores_for_max(b, u + 1, 0, 2)
                        scores_for_max(b, u + 1, 1, 0)
                    fill(u, 1)
                    scores_t(b, u, 0, 2)
                    scores_t(b, u, 1, 0)
                    if ahead:
                        scores_for_max(b, u + 1, 1, 1)
                        scores_for_max(b, u + 1, 1, 2)
                    fill(u, 2)
                    weighted_values(b, u, 0)
                    scores_t(b, u, 1, 1)
                    scores_t(b, u, 1, 2)
                    fill(u, 3)
                    weighted_values(b, u, 1)
                    if ahead:
                        transpose_max(b, u + 1)
                turn_y(b, 0)
                turn_y(b, 1)
                for i in range(NT):
                    if more and i < 3:
                        scores_for_max(b + 1, 0, (2 * i) // 3, (2 * i) % 3)
                        scores_for_max(b + 1, 0, (2 * i + 1) // 3, (2 * i + 1) % 3)
                    out_product(b, i, more)
                    if i + 2 < NT:
                        turn_y(b, i + 2)
                if more:
                    transpose_max(b + 1, 0)

            per_batch(pe, body)

        @block.scalar
        def _(act):
            act.dma_start(gates[:, 0:1], g_xattn.partition_broadcast(P)).then_inc(s_small, 16)
            act.dma_start(gates[:, 1:2], g_ffn.partition_broadcast(P)).then_inc(s_small, 16)
            act.dma_start(wsr[:, 0, :], w_std.partition_broadcast(P)).then_inc(s_small, 16)
            act.dma_start(wsr[:, 1, :], w_rec.partition_broadcast(P)).then_inc(s_small, 16)
            act.wait_ge(s_small, 64)
            act.activation(gates[:], gates[:], ACT.Tanh).then_inc(s_tanh, 1)

            def turned_hi(k, n):
                act.wait_ge(s_turn, 12 * n + k + 1)
                dst = (wt_hi if k < NT else xt_hi)[:, :, P * (k % 4):P * (k % 4) + P]
                act.activation(dst, turn_bank[:].rearrange("p (k c) -> p k c", k=NK), ACT.Copy).then_inc(s_thi, 1)

            def qk_split_hi(w, g, n, first=False):
                if not first and w == 0:
                    for s in (2 * g % SLOTS, 2 * g % SLOTS + 1):
                        act.wait_ge(s_stack[s], 192 * (2 * n + g // 2))
                act.wait_ge(s_qk, 8 * n + 2 * g + w + 1)
                act.activation(qk_hi[:, g % 2, w, :], mm_bank[w][:], ACT.Copy).then_inc(s_qkhi, 1)

            def side(kind, i, n):
                if kind in "WXH":
                    turned_hi("WXH".index(kind) * NT + i, n)
                elif kind == "V":
                    act.wait_ge(s_v, NT * n + i + 1)
                    act.activation(v_aug[:, i, :, 0:D], mm_bank[i % 2][:].rearrange("p (h d) -> p h d", h=H),
                                   ACT.Copy).then_inc(s_vcopy, 1)
                elif kind in "qkQK":
                    qk_split_hi(0 if kind in "qQ" else 1, i, n)

            def negate_max(n, u):
                s = u % SLOTS
                act.wait_ge(s_mt, 8 * n + u + 1)
                act.activation(neg_max[:], max_bank[0][0:8, 0:P], ACT.Copy, scale=-1.0).then_inc(s_neg, 1)
                act.wait_ge(s_neg, 8 * n + u + 1)
                act.dma_start(q_stack[96:97, s, :, :].rearrange("p j (i t) -> p (j i) t", i=NT).bitcast(FP32),
                              neg_max[:].bitcast(FP32)).then_inc(s_negrow[s], 16)

            def exponentials(b, u, j, k):
                act.wait_ge(s_st, 48 * b + 6 * u + 3 * j + k + 1)
                act.activation(prob[j][:, UNIT_COL[k]:UNIT_COL[k] + UNIT_LEN[k]],
                               exp_bank[(3 * j + k) % 2][:, 0:UNIT_LEN[k]], ACT.Exp, scale=SCALE).then_inc(s_exp, 1)

            for k in range(NK):
                act.wait_ge(s_wscaled, k + 1)
                raw = work[:, NF * (k % 3):NF * (k % 3) + NF]
                act.activation(w_hi[:, k, 0:2 * C].rearrange("p (h e) -> p h e", e=D)[:, :, 0:DS],
                               raw[:, 0:2 * H * DS].rearrange("p (h e) -> p h e", e=DS), ACT.Copy)
                act.activation(w_hi[:, k, 0:2 * C].rearrange("p (h e) -> p h e", e=D)[:, :, DS:D],
                               tails.rearrange("p q h e -> p (q h) e"), ACT.Copy)
                act.activation(w_hi[:, k, 2 * C:NF], raw[:, 2 * H * DS:2 * H * DS + C], ACT.Copy).then_inc(s_whi, 1)
                turned_hi(k, 0)
            for k in range(4, 8):
                turned_hi(k, 0)
            act.wait_ge(s_wload[NK], 16)
            act.activation(wp_hi[:], work[:, NF:NF + NK * C].rearrange("p (k c) -> p k c", k=NK),
                           ACT.Copy).then_inc(s_whi, 1)
            for k in range(8, 12):
                turned_hi(k, 0)
            for g in range(2):
                qk_split_hi(0, g, 0, first=True)
                qk_split_hi(1, g, 0, first=True)
            negate_max(0, 0)

            def body(b, more):
                def fill(u, gap):
                    for kind, i in pieces(FILL[u][gap], more):
                        side(kind, i, b if kind in "VQK" else b + 1)

                for u in range(STEPS):
                    fill(u, 0)
                    exponentials(b, u, 0, 0)
                    exponentials(b, u, 0, 1)
                    fill(u, 1)
                    exponentials(b, u, 0, 2)
                    exponentials(b, u, 1, 0)
                    fill(u, 2)
                    exponentials(b, u, 1, 1)
                    exponentials(b, u, 1, 2)
                    fill(u, 3)
                    if u + 1 < STEPS:
                        negate_max(b, u + 1)
                for i in range(NT):
                    act.wait_ge(s_yt, NT * b + i + 1)
                    act.activation(wt_hi[:, :, P * i:P * i + P], turn_bank[:].rearrange("p (k c) -> p k c", k=NK),
                                   ACT.Copy).then_inc(s_yhi, 1)
                if more:
                    negate_max(b + 1, 0)

            per_batch(act, body)

        @block.vector
        def _(dve):
            chain = Chain(dve, s_dve)

            def x_tile(n, i):
                return x_all[:, n % 2, i, :] if isinstance(n, int) else x_all[:, bass.ds(n % 2, 1), i, :]

            def like_x(ap, n):
                return ap if isinstance(n, int) else ap.unsqueeze(1)

            def ctx_maxima(n):
                for i in range(NT):
                    dve.wait_ge(s_ctxload[i], 16 * n + 16)
                    last = dve.tensor_reduce(w_amax[:, NK * i:NK * i + NK],
                                             ctx_raw[:, i, :].rearrange("p (k c) -> p k c", k=NK),
                                             AX.X, ALU.max, apply_absolute_value=True)
                last.then_inc(s_amax, 1)

            def scales(amax, up, down, eps):
                chain(dve.tensor_scalar(down, amax, eps, None, ALU.max))
                chain(dve.reciprocal(up, down))
                dve.tensor_scalar(up, up, FP8_MAX, None, ALU.mult)
                return dve.tensor_scalar(down, down, 1.0 / FP8_MAX, None, ALU.mult)

            def ctx_scales(n):
                dve.wait_ge(s_top, n + 1)
                scales(w_top[:], w_up[:], w_down[:], W_EPS).then_inc(s_wscale, 1)

            def x_stats(n):
                for i in range(NT):
                    wait_apart(dve, s_xload[i], 16 * n + 16)
                    last = dve.bn_stats(bn1[:, i, :], x_tile(n, i))
                chain(last, wait_apart)
                for i in range(NT):
                    last = dve.bn_aggr(mv1[:, i, :], bn1[:, i, :])
                last.then_inc(s_var1, 1)

            def layernorm_x(n, i):
                k = NT + i
                if i == 0:
                    dve.wait_ge(s_rstd1, n + 1)
                dve.wait_ge(s_turn, 12 * n + i + 1)
                buf = tile_buf[:, k % 4, :]
                chain(dve.tensor_scalar(like_x(buf, n), x_tile(n, i), mv1[:, i, 0:1], rstd1[:, i:i + 1],
                                        ALU.subtract, ALU.mult))
                chain(dve.tensor_reduce(x_amax[:, i, :], buf.rearrange("p (k c) -> p k c", k=NK),
                                        AX.X, ALU.max, apply_absolute_value=True))
                scales(x_amax[:, i, :], x_up[:, i, :], x_down[:, i, :], ACT_EPS).then_inc(s_xscale, 1)

            def rounding(n, k):
                dve.wait_ge(s_scaled, 8 * n + k + 1)
                m = magic[:, k % 2, :]
                chain(dve.tensor_scalar(m.bitcast(U16), tile_buf[:, k % 4, :].bitcast(U16)[:, 1::2],
                                        EXPONENT_BITS, None, ALU.bitwise_and))
                dve.tensor_scalar(m, m, MIN_NORMAL, MAGIC, ALU.max, ALU.mult).then_inc(s_magic, 1)

            def turned_lo(k, n):
                dve.wait_ge(s_thi, 12 * n + k + 1)
                hi, lo = (wt_hi, wt_lo) if k < NT else (xt_hi, xt_lo)
                cols = slice(P * (k % 4), P * (k % 4) + P)
                dve.tensor_tensor(lo[:, :, cols], turn_bank[:].rearrange("p (k c) -> p k c", k=NK),
                                  hi[:, :, cols].bitcast(FP32), ALU.subtract).then_inc(s_tlo, 1)

            def residual(n, i):
                dve.wait_ge(s_cross, NT * n + i + 1)
                chain(dve.scalar_tensor_tensor(x_tile(n, i), like_x(mm_bank[i % 2][:], n), gates[:, 0:1],
                                               x_tile(n, i), ALU.mult, ALU.add), wait_apart)
                chain(dve.bn_stats(bn2[:, i, :], x_tile(n, i)), wait_apart)
                dve.bn_aggr(mv2[:, i, :], bn2[:, i, :]).then_inc(s_x1, 1)

            def layernorm_x1(n, i):
                if i % 2 == 0:
                    dve.wait_ge(s_rstd2, 2 * n + i // 2 + 1)
                dve.wait_ge(s_turn, 12 * n + NT + i + 1)
                dve.tensor_scalar(like_x(tile_buf[:, i, :], n), x_tile(n, i), mv2[:, i, 0:1],
                                  rstd2[:, i:i + 1], ALU.subtract, ALU.mult).then_inc(s_hn, 1)

            def qk_split_lo(w, g, n):
                dve.wait_ge(s_qkhi, 8 * n + 2 * g + w + 1)
                dve.tensor_tensor(qk_lo[:, g % 2, w, :], mm_bank[w][:], qk_hi[:, g % 2, w, :].bitcast(FP32),
                                  ALU.subtract).then_inc(s_qklo, 1)

            def side(kind, i, n):
                if kind in "WXH":
                    turned_lo("WXH".index(kind) * NT + i, n)
                elif kind == "S":
                    residual(n, i)
                elif kind in "qkQK":
                    qk_split_lo(0 if kind in "qQ" else 1, i, n)

            def maxima(n, u, j, k):
                unit = 3 * j + k
                dve.wait_ge(s_sm, 48 * n + 6 * u + unit + 1)
                for i, col in MAX_UNITS[k]:
                    last = dve.tensor_reduce(row_max[:, NT * j + i:NT * j + i + 1],
                                             max_bank[unit % 2][:, col:col + P * (i + 1)], AX.X, ALU.max)
                last.then_inc(s_max, 1)

            def normalise(b, u):
                dve.wait_ge(s_pv, 16 * b + 2 * u + 2)
                pv = pv_bank[:, 0:8 * (D + 1)].rearrange("p (j i e) -> p j i e", j=2, i=NT)
                rd = rden[:].rearrange("p (j i) -> p j i", j=2)
                chain(dve.reciprocal(rd, pv[:, :, :, D]))
                dve.tensor_tensor(y[:, :, 2 * D * u:2 * D * u + 2 * D].rearrange("p i (j d) -> p j i d", j=2),
                                  pv[:, :, :, 0:D], rd.unsqueeze(3).broadcast_to([P, 2, NT, D]),
                                  ALU.mult).then_inc(s_norm, 1)

            def weight_chunk(k):
                raw = work[:, NF * (k % 3):NF * (k % 3) + NF]
                dve.wait_ge(s_wload[k], 16)
                std = raw[:, 0:2 * H * DS].rearrange("p (q h e) -> p q h e", q=2, h=H)
                v0 = 2 * H * DS
                low = raw[:, v0 + C:NF].rearrange("p (q h e) -> p q h e", q=2, h=H)
                for q in range(2):
                    dve.tensor_tensor(std[:, q], std[:, q],
                                      wsr_root[:, 0, :].unsqueeze(2).broadcast_to([P, H, DS]), ALU.mult)
                    last = dve.tensor_tensor(low[:, q], low[:, q],
                                             wsr_root[:, 1, :].unsqueeze(2).broadcast_to([P, H, R]), ALU.mult)
                chain(last)
                if k:
                    dve.wait_ge(s_whi, k)
                chain(dve.tensor_copy(tails, low))
                dve.copy_predicated(tails[:, 0], swap, low[:, 1])
                dve.copy_predicated(tails[:, 1], swap, low[:, 0]).then_inc(s_wscaled, 1)
                dve.wait_ge(s_whi, k + 1)
                hi = w_hi[:, k, :].bitcast(FP32)
                qk = w_lo[:, k, 0:2 * C].rearrange("p (h e) -> p h e", e=D)
                qk_h = hi[:, 0:2 * C].rearrange("p (h e) -> p h e", e=D)
                dve.tensor_tensor(qk[:, :, 0:DS], raw[:, 0:v0].rearrange("p (h e) -> p h e", e=DS),
                                  qk_h[:, :, 0:DS], ALU.subtract)
                dve.tensor_tensor(qk[:, :, DS:D], tails.rearrange("p q h e -> p (q h) e"),
                                  qk_h[:, :, DS:D], ALU.subtract)
                dve.tensor_tensor(w_lo[:, k, 2 * C:NF], raw[:, v0:v0 + C], hi[:, 2 * C:NF],
                                  ALU.subtract).then_inc(s_wlo, 1)

            x_stats(0)
            ctx_maxima(0)
            dve.wait_ge(s_root, 1)
            chain(dve.tensor_scalar(swap, wsr[:, 1, :].unsqueeze(2).broadcast_to([P, H, R]), 0.1, None, ALU.is_gt))
            ctx_scales(0)
            rounding(0, 0)
            rounding(0, 1)
            weight_chunk(0)
            turned_lo(0, 0)
            rounding(0, 2)
            weight_chunk(1)
            turned_lo(1, 0)
            layernorm_x(0, 0)
            rounding(0, 3)
            weight_chunk(2)
            turned_lo(2, 0)
            layernorm_x(0, 1)
            rounding(0, 4)
            weight_chunk(3)
            turned_lo(3, 0)
            layernorm_x(0, 2)
            rounding(0, 5)
            turned_lo(4, 0)
            layernorm_x(0, 3)
            rounding(0, 6)
            turned_lo(5, 0)
            rounding(0, 7)
            turned_lo(6, 0)
            turned_lo(7, 0)
            dve.wait_ge(s_whi, NK + 1)
            dve.tensor_tensor(wp_lo[:], work[:, NF:NF + NK * C].rearrange("p (k c) -> p k c", k=NK),
                              wp_hi[:].bitcast(FP32), ALU.subtract).then_inc(s_wlo, 1)
            dve.wait_ge(s_tanh, 1)
            for i in range(NT):
                residual(0, i)
            for i in range(NT):
                layernorm_x1(0, i)
                turned_lo(8 + i, 0)
            for g in range(2):
                qk_split_lo(0, g, 0)
                qk_split_lo(1, g, 0)
            for unit in range(6):
                maxima(0, 0, unit // 3, unit % 3)
            first = chain.n
            dve.sem_inc(s_outt, FIRST_OUT)

            own = {(0, 0): [(ctx_maxima, ())], (0, 1): [(x_stats, ())], (0, 2): [(ctx_scales, ())],
                   (0, 3): [(rounding, (0,))],
                   (1, 0): [(rounding, (1,))], (1, 1): [(layernorm_x, (0,))], (1, 2): [(rounding, (2,))],
                   (1, 3): [(layernorm_x, (1,))],
                   (2, 0): [(rounding, (3,))], (2, 1): [(rounding, (4,))], (2, 3): [(layernorm_x, (2,))],
                   (3, 0): [(layernorm_x, (3,))], (3, 1): [(rounding, (5,))], (3, 2): [(rounding, (6,))],
                   (3, 3): [(rounding, (7,))],
                   (5, 0): [(layernorm_x1, (0,)), (layernorm_x1, (1,))],
                   (5, 3): [(layernorm_x1, (2,)), (layernorm_x1, (3,))]}

            def body(b, more):
                n = b + 1
                chain.at(first + DVE_CHAIN * b)

                def fill(u, gap):
                    for kind, i in pieces(FILL[u][gap], more):
                        side(kind, i, b if kind in "VQK" else n)
                    for f, a in own.get((u, gap), []) if more else []:
                        f(n, *a)

                for u in range(STEPS):
                    for gap in range(4):
                        if u + 1 < STEPS and gap < 3:
                            for unit in (2 * gap, 2 * gap + 1):
                                maxima(b, u + 1, unit // 3, unit % 3)
                        fill(u, gap)
                    normalise(b, u)

                def y_lo(i):
                    dve.wait_ge(s_yhi, NT * b + i + 1)
                    dve.tensor_tensor(wt_lo[:, :, P * i:P * i + P], turn_bank[:].rearrange("p (k c) -> p k c", k=NK),
                                      wt_hi[:, :, P * i:P * i + P].bitcast(FP32), ALU.subtract).then_inc(s_ylo, 1)

                y_lo(0)
                y_lo(1)
                for i in range(NT):
                    if more and i < 3:
                        for unit in (2 * i, 2 * i + 1):
                            maxima(n, 0, unit // 3, unit % 3)
                    if i + 2 < NT:
                        y_lo(i + 2)
                    dve.wait_ge(s_wpmm, NT * b + i + 1)
                    dve.scalar_tensor_tensor(x_tile(b, i), like_x(mm_bank[i % 2][:], b), gates[:, 1:2],
                                             x_tile(b, i), ALU.mult, ALU.add).then_inc(s_outt, 1)
                if more:
                    assert chain.n == DVE_CHAIN, chain.n

            per_batch(dve, body)


_INS = ["x", "ctx_2048", "g_xattn", "g_ffn", "L0_ffn_Wa", "L0_ffn_Wp", "L0_ffn_w_std", "L0_ffn_w_rec"]


def kernel(**inputs):
    import numpy as np
    import concourse.bacc as bacc
    from concourse.bass_utils import run_bass_kernel_spmd

    nc = bacc.Bacc("TRN2", target_bir_lowering=False, num_devices=1)
    arrays, args = {}, []
    for name in _INS:
        a = np.ascontiguousarray(inputs[name])
        arrays[f"in_{name}"] = a
        args.append(nc.dram_tensor(f"in_{name}", a.shape, mybir.dt.from_np(a.dtype), kind="ExternalInput").ap())
    out = nc.dram_tensor("out", (B, T, C), FP32, kind="ExternalOutput").ap()
    flamingo_block(nc, *args, out)
    r = run_bass_kernel_spmd(nc, [arrays], core_ids=[0])
    return r.results[0]["out"]
```

```python
import concourse.bass as bass
from concourse import mybir
from concourse.alu_op_type import AluOpType as ALU
from contextlib import ExitStack

FP32 = mybir.dt.float32
FP32R = mybir.dt.float32r
BF16 = mybir.dt.bfloat16
U16 = mybir.dt.uint16
U32 = mybir.dt.uint32
ACT = mybir.ActivationFunctionType
AX = mybir.AxisListType

B, T, C = 4, 512, 512
H, D, R = 16, 32, 8
DS = D - R
P = 128
PV_ROWS = 64 + D + 1
NT = T // P
NK = C // P
NF = 3 * C
STEPS = H // 2
SLOTS = 4
SCALE = float(D) ** -0.5
FP8_MAX, ACT_EPS, W_EPS, LN_EPS = 448.0, 1e-4, 1e-6, 1e-5
MAGIC, MIN_NORMAL, EXPONENT_BITS = 1.5 * 2.0 ** 20, 2.0 ** -6, 0x7F80

MAX_UNITS = [[(3, 0)], [(2, 0), (0, 384)], [(1, 0)]]
EXP_UNITS = [[(0, 0)], [(1, 0), (3, 384)], [(2, 0)]]
PROB_COL = [0, 512, 1024, 896]
UNIT_COL = [0, 512, 1024]
UNIT_LEN = [512, 512, 256]

FILL = [
    ["Q2", "K2", "", ""],
    ["Q3", "W0", "W1", ""],
    ["K3", "W2", "W3", ""],
    ["X0", "X1", "", "S0"],
    ["S1", "X2", "X3", "S2"],
    ["S3", "H0", "H1", ""],
    ["H2", "H3", "q0", "k0"],
    ["q1", "k1", "", ""],
]
TURNED = [sum(name[0] in "WXH" for v in range(u + 1) for gap in FILL[v][0:3 if v == u else 4] for name in gap.split())
          for u in range(STEPS)]
DVE_CHAIN, POOL_CHAIN = 43, 19


def pieces(gap, more):
    for name in gap.split():
        if more or name[0] in "VQK":
            yield name[0], int(name[1])


class Chain:

    def __init__(self, eng, sem):
        self.eng, self.sem, self.base, self.n = eng, sem, 0, 0

    def __call__(self, ins, wait=lambda eng, sem, count: eng.wait_ge(sem, count)):
        self.n += 1
        ins.then_inc(self.sem, 1)
        wait(self.eng, self.sem, self.base + self.n)

    def at(self, base):
        self.base, self.n = base, 0


def flamingo_block(nc, x, ctx, g_xattn, g_ffn, wa, wp, w_std, w_rec, out):
    es = ExitStack()
    with es:
        def sb(name, shape, dt=FP32):
            return es.enter_context(nc.sbuf_tensor(name, shape, dt))

        def pb(name, dt=FP32):
            return es.enter_context(nc.psum_tensor(name, [P, 512], dt))

        def sem(name):
            return es.enter_context(nc.semaphore(name))

        w_hi, w_lo = sb("w_hi", [P, NK, NF], FP32R), sb("w_lo", [P, NK, NF], FP32R)
        wp_hi, wp_lo = sb("wp_hi", [P, NK, C], FP32R), sb("wp_lo", [P, NK, C], FP32R)
        q_stack = sb("q_stack", [97, SLOTS, 2, T], FP32R)
        k_stack = sb("k_stack", [97, SLOTS, 2, T], FP32R)
        qk_hi = sb("qk_hi", [P, 2, 2, T], FP32R)
        qk_lo = sb("qk_lo", [P, 2, 2, T], FP32R)
        xt_hi, xt_lo = sb("xt_hi", [P, NK, T], FP32R), sb("xt_lo", [P, NK, T], FP32R)
        wt_hi, wt_lo = sb("wt_hi", [P, NK, T], FP32R), sb("wt_lo", [P, NK, T], FP32R)
        x_all = sb("x_all", [P, 2, NT, C])
        ctx_raw = sb("ctx_raw", [P, NT, C])
        tile_buf = sb("tile_buf", [P, 4, C])
        v_aug = sb("v_aug", [P, NT, H, D + 1])
        work = sb("work", [P, 4608])
        prob = [work[:, 0:1280], work[:, 1280:2560]]
        y = work[:, 2560:4608].rearrange("p (i c) -> p i c", i=NT)
        values = sb("values", [P, T])

        def magic(n, k):
            place = values[:, 256 * (k % 2):256 * (k % 2) + 256] if isinstance(n, int) else y[:, k % 2, 256:512]
            return place.bitcast(BF16)

        ident = sb("ident", [P, P])
        ident_bf = sb("ident_bf", [P, P], BF16)
        future = sb("future", [P, P], BF16)
        gates = sb("gates", [P, 2])
        wsr = sb("wsr", [P, 2, H])
        wsr_root = sb("wsr_root", [P, 2, H])
        neg_half = sb("neg_half", [P, NT])
        spare = x_all[:, 1, 0, :]
        tails = spare[:, 0:2 * H * R].rearrange("p (q h e) -> p q h e", q=2, h=H)
        swap = spare[:, 256:256 + H * R].bitcast(U32).rearrange("p (h e) -> p h e", h=H)
        half = spare[:, 384:384 + 2 * H].rearrange("p (q h) -> p q h", q=2)
        w_amax, w_top = sb("w_amax", [P, NT * NK]), sb("w_top", [P, NT * NK])
        w_up, w_down = sb("w_up", [P, NT * NK]), sb("w_down", [P, NT * NK])
        x_amax = sb("x_amax", [P, NT, NK])
        x_up, x_down = sb("x_up", [P, NT, NK]), sb("x_down", [P, NT, NK])
        bn1, mv1 = sb("bn1", [P, NT, 6]), sb("mv1", [P, NT, 2])
        bn2, mv2 = sb("bn2", [P, NT, 6]), sb("mv2", [P, NT, 2])
        rstd1, rstd2 = sb("rstd1", [P, NT]), sb("rstd2", [P, NT])
        row_max = sb("row_max", [P, 8])
        neg_max = sb("neg_max", [8, P], FP32R)
        rden = sb("rden", [P, 8])

        max_bank = [pb("max_bank0"), pb("max_bank1")]
        exp_bank = [pb("exp_bank0"), pb("exp_bank1")]
        pv_bank = pb("pv_bank")
        turn_bank = pb("turn_bank")
        turned_max = turn_bank[0:8, 0:P]
        mm_bank = [pb("mm_bank0"), pb("mm_bank1")]
        y_bank = [exp_bank[0], exp_bank[1], turn_bank, exp_bank[0]]

        s_begun = sem("s_begun")
        s_const = sem("s_const")
        s_cleared = sem("s_cleared")
        s_small = sem("s_small")
        s_tanh = sem("s_tanh")
        s_root = sem("s_root")
        s_wload = [sem(f"s_wload{i}") for i in range(NK + 1)]
        s_wscaled = sem("s_wscaled")
        s_whi = sem("s_whi")
        s_wlo = sem("s_wlo")
        s_xload = [sem(f"s_xload{i}") for i in range(NT)]
        s_ctxload = [sem(f"s_ctxload{i}") for i in range(NT)]
        s_amax = sem("s_amax")
        s_top = sem("s_top")
        s_wscale = sem("s_wscale")
        s_var1, s_rstd1 = sem("s_var1"), sem("s_rstd1")
        s_rstd2 = sem("s_rstd2")
        s_xscale = sem("s_xscale")
        s_scaled = sem("s_scaled")
        s_magic = sem("s_magic")
        s_quant = sem("s_quant")
        s_hn = sem("s_hn")
        s_turn = sem("s_turn")
        s_thi, s_tlo = sem("s_thi"), sem("s_tlo")
        s_cross, s_x1 = sem("s_cross"), sem("s_x1")
        s_qk, s_qkhi, s_qklo = sem("s_qk"), sem("s_qkhi"), sem("s_qklo")
        s_v, s_vcopy = sem("s_v"), sem("s_vcopy")
        s_stack = [sem(f"s_stack{i}") for i in range(SLOTS)]
        s_negrow = [sem(f"s_negrow{i}") for i in range(SLOTS)]
        s_sm, s_max = sem("s_sm"), sem("s_max")
        s_mt, s_neg = sem("s_mt"), sem("s_neg")
        s_st, s_exp = sem("s_st"), sem("s_exp")
        s_causal = sem("s_causal")
        s_pv = sem("s_pv")
        s_pvcopy, s_pvt = sem("s_pvcopy"), sem("s_pvt")
        s_norm = sem("s_norm")
        s_yt, s_yhi, s_ylo = sem("s_yt"), sem("s_yhi"), sem("s_ylo")
        s_wpmm = sem("s_wpmm")
        s_outt = sem("s_outt")
        s_store = sem("s_store")
        s_dve = sem("s_dve")
        s_pool = sem("s_pool")

        FIRST_OUT = NT

        def wait_apart(eng, sem, count):
            if not isinstance(count, int):
                count = eng.to_reg(count)
                eng.wait_ge(s_begun, 1)
            eng.wait_ge(sem, count)

        def per_batch(eng, body):
            with eng.Fori(0, B - 1) as b:
                body(b, True)
            body(B - 1, False)

        block = es.enter_context(nc.Block())

        @block.sync
        def _(sp):
            x_v = x.rearrange("b (i p) c -> b i p c", p=P)
            ctx_v = ctx.rearrange("b (i p) c -> b i p c", p=P)
            out_v = out.rearrange("b (i p) c -> b i p c", p=P)

            def load_tiles(n, parity):
                for i in range(NT):
                    sp.dma_start(x_all[:, parity, i, :], x_v[n, i, :, :]).then_inc(s_xload[i], 16)

            def load_ctx(n):
                for i in range(NT):
                    if isinstance(n, int):
                        src, dst = ctx_v[n, i, :, :], ctx_raw[:, i, :]
                    else:
                        src, dst = ctx_v[bass.ds(n, 1), i, :, :].rearrange("a p c -> p a c"), ctx_raw[:, i:i + 1, :]
                    sp.dma_start(dst, src).then_inc(s_ctxload[i], 16)

            def stack(n, u, first=False):
                g, s = u // 2, u % SLOTS
                wait_apart(sp, s_qklo, 8 * n + 2 * g + 2)
                if not first:
                    wait_apart(sp, s_st, 48 * n + 6 * (u - SLOTS) + 6)
                for j in range(2):
                    rows = slice(D * (2 * (u % 2) + j), D * (2 * (u % 2) + j) + D)
                    for dst, w, parts in ((q_stack, 0, (qk_hi, qk_lo, qk_hi)),
                                          (k_stack, 1, (qk_hi, qk_hi, qk_lo))):
                        for a, part in enumerate(parts):
                            sp.dma_start(dst[D * a:D * a + D, s, j, :].bitcast(FP32),
                                         part[rows, g % 2, w, :].bitcast(FP32)).then_inc(s_stack[s], 16)

            load_tiles(0, 0)
            load_ctx(0)
            wa_v = wa.rearrange("(k p) f -> p k f", p=P)
            for k in range(NK):
                if k == NK - 1:
                    sp.wait_ge(s_wlo, 1)
                sp.dma_start(work[:, NF * (k % 3):NF * (k % 3) + NF], wa_v[:, k, :]).then_inc(s_wload[k], 16)
            sp.wait_ge(s_wlo, 3)
            sp.dma_start(work[:, NF:NF + NK * C].rearrange("p (k c) -> p k c", k=NK),
                         wp.rearrange("(k p) c -> p k c", p=P)).then_inc(s_wload[NK], 16)
            sp.wait_ge(s_scaled, NT)
            load_ctx(1)
            for u in range(SLOTS):
                stack(0, u, first=True)

            def body(b, more, ctx_more):
                if more:
                    for i in range(NT):
                        if isinstance(b, int):
                            dst, src = x_all[:, (b + 1) % 2, i, :], x_v[b + 1, i, :, :]
                        else:
                            dst = x_all[:, bass.ds((b + 1) % 2, 1), i, :]
                            src = x_v[bass.ds(b + 1, 1), i, :, :].rearrange("a p c -> p a c")
                        sp.dma_start(dst, src).then_inc(s_xload[i], 16)
                for u in range(SLOTS, STEPS):
                    stack(b, u)
                if ctx_more:
                    wait_apart(sp, s_scaled, 8 * b + 8 + NT)
                    load_ctx(b + 2)
                if more:
                    for u in range(SLOTS):
                        stack(b + 1, u)
                for i in range(NT):
                    wait_apart(sp, s_outt, FIRST_OUT + NT * b + i + 1)
                    if not isinstance(b, int):
                        sp.dma_start(out_v[bass.ds(b, 1), i, :, :].rearrange("a p c -> p a c"),
                                     x_all[:, bass.ds(b % 2, 1), i, :]).then_inc(s_store, 16)
                    else:
                        sp.dma_start(out_v[b, i, :, :], x_all[:, b % 2, i, :]).then_inc(s_store, 16)
                wait_apart(sp, s_store, 16 * NT * b + 16 * NT)

            with sp.Fori(0, B - 2) as b:
                body(b, True, True)
            body(B - 2, True, False)
            body(B - 1, False, False)

        @block.gpsimd
        def _(pool):
            chain = Chain(pool, s_pool)
            pool.memset(neg_half[:], -0.5).then_inc(s_begun, 1)
            chain(pool.memset(ident[:], 0.0))
            chain(pool.affine_select(out=ident[:], in_=ident[:], compare_op=ALU.not_equal, fill=1.0,
                                     base=0, pattern=[[-1, P]], channel_multiplier=1))
            pool.tensor_copy(ident_bf[:], ident[:]).then_inc(s_const, 1)
            chain(pool.memset(future[:], 0.0))
            pool.affine_select(out=future[:], in_=future[:], compare_op=ALU.is_ge, fill=-3.0e38,
                               base=0, pattern=[[-1, P]], channel_multiplier=1).then_inc(s_const, 1)
            pool.wait_ge(s_const, 2)
            pool.memset(k_stack[96:97, :, :, :].bitcast(FP32), 1.0).then_inc(s_const, 1)
            pool.wait_ge(s_const, 3)
            chain(pool.memset(half, 0.5))
            pool.wait_ge(s_small, 64)
            chain(pool.tensor_scalar(wsr_root[:], wsr[:], 1e-8, None, ALU.max))
            chain(pool.tensor_tensor(wsr_root[:], wsr_root[:], half, ALU.pow))
            pool.memset(v_aug[:, :, :, D:D + 1], 1.0).then_inc(s_root, 1)

            def top(n):
                wait_apart(pool, s_amax, n + 1)
                pool.partition_all_reduce(w_top[:], w_amax[:], P, bass.bass_isa.ReduceOp.max).then_inc(s_top, 1)

            def inv_std(n, mv, rstd, lo, hi, var_sem, rstd_sem, count):
                wait_apart(pool, var_sem, count)
                chain(pool.tensor_scalar(rstd[:, lo:hi], mv[:, lo:hi, 1], LN_EPS, None, ALU.add))
                pool.tensor_tensor(rstd[:, lo:hi], rstd[:, lo:hi], neg_half[:, lo:hi], ALU.pow).then_inc(rstd_sem, 1)

            def inv_std1(n):
                inv_std(n, mv1, rstd1, 0, NT, s_var1, s_rstd1, n + 1)

            def inv_std2(n, pair):
                inv_std(n, mv2, rstd2, 2 * pair, 2 * pair + 2, s_x1, s_rstd2, NT * n + 2 * pair + 2)

            def blocks(ap):
                return ap.rearrange("p (k c) -> p k c", k=NK)

            def spread(scales):
                return scales.unsqueeze(2).broadcast_to([P, NK, P])

            def scale_up(n, k):
                buf = tile_buf[:, k % 4, :]
                if k < NT:
                    if k == 0:
                        pool.wait_ge(s_wscale, n + 1)
                    src, up = ctx_raw[:, k, :], w_up[:, NK * k:NK * k + NK]
                else:
                    pool.wait_ge(s_xscale, NT * n + k - NT + 1)
                    src, up = buf, x_up[:, k - NT, :]
                pool.tensor_tensor(blocks(buf), blocks(src), spread(up), ALU.mult).then_inc(s_scaled, 1)

            def quantise(n, k):
                buf = tile_buf[:, k % 4, :]
                down = w_down[:, NK * k:NK * k + NK] if k < NT else x_down[:, k - NT, :]
                pool.wait_ge(s_magic, 8 * n + k + 1)
                chain(pool.tensor_tensor(buf, buf, magic(n, k), ALU.add))
                chain(pool.tensor_tensor(buf, buf, magic(n, k), ALU.subtract))
                pool.tensor_tensor(blocks(buf), blocks(buf), spread(down), ALU.mult).then_inc(s_quant, 1)

            def zero_future(b, u, j):
                wait_apart(pool, s_exp, 48 * b + 6 * u + 3 * j + 3)
                three = prob[j].rearrange("p (a c) -> p a c", c=256)[:, 0:5:2, 0:P]
                pool.affine_select(out=three, in_=three, compare_op=ALU.is_ge, fill=0.0,
                                   base=0, pattern=[[0, 3], [1, P]], channel_multiplier=-1)
                fourth = prob[j][:, PROB_COL[3]:PROB_COL[3] + P]
                last = pool.affine_select(out=fourth, in_=fourth, compare_op=ALU.is_ge, fill=0.0,
                                          base=0, pattern=[[1, P]], channel_multiplier=-1)
                if j:
                    last.then_inc(s_causal, 1)

            top(0)
            inv_std1(0)
            scale_up(0, 0)
            scale_up(0, 1)
            for k in range(8):
                quantise(0, k)
                if k + 2 < 8:
                    scale_up(0, k + 2)
            inv_std2(0, 0)
            inv_std2(0, 1)
            first = chain.n

            def body(b, more):
                n = b + 1
                chain.at(first + POOL_CHAIN * b)
                before = {0: [(top, ()), (scale_up, (0,)), (scale_up, (1,))]}
                after = {0: [(quantise, (0,)), (scale_up, (2,)), (inv_std1, ()), (quantise, (1,)), (scale_up, (3,))],
                         1: [(quantise, (2,)), (quantise, (3,)), (scale_up, (4,)), (scale_up, (5,))],
                         2: [(quantise, (4,)), (quantise, (5,)), (scale_up, (6,)), (scale_up, (7,))],
                         3: [(quantise, (6,)), (quantise, (7,))],
                         4: [(inv_std2, (0,))],
                         5: [(inv_std2, (1,))]}
                for u in range(STEPS):
                    for f, a in before.get(u, []) if more else []:
                        f(n, *a)
                    zero_future(b, u, 0)
                    zero_future(b, u, 1)
                    for f, a in after.get(u, []) if more else []:
                        f(n, *a)
                if more:
                    assert chain.n == POOL_CHAIN, chain.n

            per_batch(pool, body)

        @block.tensor
        def _(pe):
            def split_product(dst, l_hi, l_lo, r_hi, r_lo, done):
                for k in range(NK):
                    pe.matmul(dst, l_hi(k), r_hi(k), start=(k == 0), stop=False)
                    pe.matmul(dst, l_hi(k), r_lo(k), start=False, stop=False)
                    last = pe.matmul(dst, l_lo(k), r_hi(k), start=False, stop=(k == NK - 1))
                last.then_inc(done, 1)

            def turn(src, done, bank=turn_bank):
                for k in range(NK):
                    last = pe.transpose(bank[:, P * k:P * k + P], src[:, P * k:P * k + P], ident[:])
                last.then_inc(done, 1)

            def rows_of(t, i):
                return lambda k: t[:, k, P * i:P * i + P]

            def cols_of(t, lo, n):
                return lambda k: t[:, k, lo:lo + n]

            def side(kind, i, n, more, first=False, negated=None):
                if negated is not None and kind in "WXH":
                    pe.wait_ge(s_neg, negated)
                if kind in "WX":
                    k = i + (NT if kind == "X" else 0)
                    pe.wait_ge(s_quant, 8 * n + k + 1)
                    if k:
                        pe.wait_ge(s_tlo, 12 * n + k)
                    turn(tile_buf[:, k % 4, :], s_turn)
                elif kind == "H":
                    pe.wait_ge(s_hn, NT * n + i + 1)
                    pe.wait_ge(s_tlo, 12 * n + 8 + i)
                    turn(tile_buf[:, i % 4, :], s_turn)
                elif kind == "S":
                    if i >= 2:
                        pe.wait_ge(s_x1, NT * n + i - 1)
                    elif not first:
                        pe.wait_ge(s_qklo, 8 * n - 1 + i)
                    pe.wait_ge(s_tlo, 12 * n + NT + i + 1)
                    split_product(mm_bank[i % 2][:], rows_of(xt_hi, i), rows_of(xt_lo, i),
                                  cols_of(wt_hi, 0, C), cols_of(wt_lo, 0, C), s_cross)
                elif kind == "V":
                    if i < 2:
                        pe.wait_ge(s_qklo, 8 * n + 3 + i)
                    else:
                        pe.wait_ge(s_vcopy, NT * n + i - 1)
                    split_product(mm_bank[i % 2][:], rows_of(xt_hi, i), rows_of(xt_lo, i),
                                  cols_of(w_hi, 2 * C, C), cols_of(w_lo, 2 * C, C), s_v)
                else:
                    w, g = (0 if kind in "qQ" else 1), i
                    if g == 0:
                        pe.wait_ge(s_x1, NT * n + 3 + w)
                    elif g == 2:
                        pe.wait_ge(s_vcopy, NT * n + 3 + w)
                        pe.wait_ge(s_outt, FIRST_OUT + NT * n - 1 + w)
                    else:
                        pe.wait_ge(s_qklo, 8 * n + 2 * g - 1 + w)
                    if g == 0:
                        pe.wait_ge(s_tlo, 12 * n + 12)
                    at = C * w + P * g
                    split_product(mm_bank[w][:], cols_of(w_hi, at, P), cols_of(w_lo, at, P),
                                  cols_of(xt_hi, 0, T), cols_of(xt_lo, 0, T), s_qk)

            def scores_for_max(n, u, j, k, first=False):
                s, unit = u % SLOTS, 3 * j + k
                if unit == 0:
                    pe.wait_ge(s_stack[s], 192 * (2 * n + u // SLOTS + 1))
                if unit >= 2 or not first:
                    pe.wait_ge(s_max, 48 * n + 6 * u + unit - 1)
                bank = max_bank[unit % 2]
                for i, col in MAX_UNITS[k]:
                    width = P * (i + 1)
                    pe.matmul(bank[:, col:col + width], q_stack[0:96, s, j, P * i:P * i + P],
                              k_stack[0:96, s, j, 0:width], start=True, stop=False)
                    last = pe.matmul(bank[:, col + P * i:col + width], ident_bf[:], future[:],
                                     start=False, stop=True)
                last.then_inc(s_sm, 1)

            def transpose_max(n, u):
                pe.wait_ge(s_max, 48 * n + 6 * u + 6)
                pe.transpose(turned_max, row_max[:], ident[:]).then_inc(s_mt, 1)

            def scores_t(b, u, j, k):
                s, unit = u % SLOTS, 3 * j + k
                if unit == 0:
                    pe.wait_ge(s_negrow[s], 16 * (2 * b + u // SLOTS + 1))
                if unit >= 2:
                    pe.wait_ge(s_exp, 48 * b + 6 * u + unit - 1)
                bank = exp_bank[unit % 2]
                for i, col in EXP_UNITS[k]:
                    last = pe.matmul(bank[:, col:col + T - P * i], k_stack[0:97, s, j, P * i:P * i + P],
                                     q_stack[0:97, s, j, P * i:T], start=True, stop=True)
                last.then_inc(s_st, 1)

            def weighted_values(b, u):
                if u == 0:
                    pe.wait_ge(s_vcopy, NT * b + NT)
                else:
                    pe.wait_ge(s_norm, 8 * b + u)
                pe.wait_ge(s_causal, 8 * b + u + 1)
                for m in range(NT):
                    for j in range(2):
                        last = pe.matmul(pv_bank[64 * j:64 * j + D + 1, P * m:T], v_aug[:, m, 2 * u + j, :],
                                         prob[j][:, PROB_COL[m]:PROB_COL[m] + T - P * m],
                                         start=(m == 0), stop=(m == NT - 1))
                last.then_inc(s_pv, 1)

            def turn_values(b, u):
                pe.wait_ge(s_pvcopy, 8 * b + u + 1)
                for i in range(NT):
                    last = pe.transpose(pv_bank[:, P * i:P * i + PV_ROWS], values[0:PV_ROWS, P * i:P * i + P],
                                        ident[0:PV_ROWS, 0:PV_ROWS])
                last.then_inc(s_pvt, 1)

            def turn_y(b, i):
                if i == 0:
                    pe.wait_ge(s_norm, 8 * b + 8)
                if i == 2:
                    pe.wait_ge(s_neg, 8 * b + 8)
                if i == 3:
                    pe.wait_ge(s_ylo, NT * b + 1)
                turn(y[:, i, :], s_yt, y_bank[i])

            def out_product(b, i, more):
                if i < 2 and more:
                    pe.wait_ge(s_vcopy, NT * b + NT + 3 + i)
                elif i < 2:
                    pe.wait_ge(s_qklo, 8 * b + 7 + i)
                else:
                    pe.wait_ge(s_outt, FIRST_OUT + NT * b + i - 1)
                pe.wait_ge(s_ylo, NT * b + i + 1)
                split_product(mm_bank[i % 2][:], rows_of(wt_hi, i), rows_of(wt_lo, i),
                              cols_of(wp_hi, 0, C), cols_of(wp_lo, 0, C), s_wpmm)

            pe.wait_ge(s_cleared, 1)
            pe.wait_ge(s_const, 1)
            for name in "W0 W1 W2 W3 X0 X1 X2 X3 S0 S1 S2 S3 H0 H1 H2 H3".split():
                side(name[0], int(name[1]), 0, True, first=True)
            pe.wait_ge(s_wlo, NK + 1)
            for g in range(2):
                side("q", g, 0, True)
                side("k", g, 0, True)
            for i in range(NT):
                side("V", i, 0, True)
            pe.wait_ge(s_const, 3)
            for unit in range(6):
                scores_for_max(0, 0, unit // 3, unit % 3, first=True)
            pe.wait_ge(s_tlo, 12)
            transpose_max(0, 0)

            def body(b, more):
                def fill(u, gap):
                    for kind, i in pieces(FILL[u][gap], more):
                        side(kind, i, b if kind in "VQK" else b + 1, more, negated=8 * b + u + 1 + gap // 3)

                def max_pair(n, u, pair):
                    for unit in (2 * pair, 2 * pair + 1):
                        scores_for_max(n, u, unit // 3, unit % 3)

                def exp_pair(u, pair):
                    for unit in (2 * pair, 2 * pair + 1):
                        scores_t(b, u, unit // 3, unit % 3)

                for u in range(STEPS):
                    ahead = u + 1 < STEPS
                    if ahead:
                        max_pair(b, u + 1, 0)
                    if u:
                        weighted_values(b, u - 1)
                    exp_pair(u, 0)
                    if ahead:
                        max_pair(b, u + 1, 1)
                    fill(u, 0)
                    if u:
                        turn_values(b, u - 1)
                    exp_pair(u, 1)
                    if ahead:
                        max_pair(b, u + 1, 2)
                    fill(u, 1)
                    exp_pair(u, 2)
                    fill(u, 2)
                    if ahead:
                        if more and TURNED[u]:
                            pe.wait_ge(s_tlo, 12 * (b + 1) + TURNED[u])
                        pe.wait_ge(s_neg, 8 * b + u + 1)
                        transpose_max(b, u + 1)
                    fill(u, 3)
                weighted_values(b, STEPS - 1)
                n = b + 1
                if more:
                    side("V", 0, n, more)
                turn_values(b, STEPS - 1)
                if more:
                    side("V", 1, n, more)
                for i in range(3):
                    turn_y(b, i)
                if more:
                    max_pair(n, 0, 0)
                    side("V", 2, n, more)
                    max_pair(n, 0, 1)
                    side("V", 3, n, more)
                    max_pair(n, 0, 2)
                turn_y(b, 3)
                out_product(b, 0, more)
                if more:
                    pe.wait_ge(s_ylo, NT * b + 3)
                    transpose_max(n, 0)
                for i in range(1, NT):
                    out_product(b, i, more)

            per_batch(pe, body)

        @block.scalar
        def _(act):
            act.dma_start(gates[:, 0:1], g_xattn.partition_broadcast(P)).then_inc(s_small, 16)
            act.dma_start(gates[:, 1:2], g_ffn.partition_broadcast(P)).then_inc(s_small, 16)
            act.dma_start(wsr[:, 0, :], w_std.partition_broadcast(P)).then_inc(s_small, 16)
            act.dma_start(wsr[:, 1, :], w_rec.partition_broadcast(P)).then_inc(s_small, 16)
            act.wait_ge(s_small, 64)
            act.activation(gates[:], gates[:], ACT.Tanh).then_inc(s_tanh, 1)

            def turned_hi(k, n):
                act.wait_ge(s_turn, 12 * n + k + 1)
                dst = (wt_hi if k < NT else xt_hi)[:, :, P * (k % 4):P * (k % 4) + P]
                act.activation(dst, turn_bank[:].rearrange("p (k c) -> p k c", k=NK), ACT.Copy).then_inc(s_thi, 1)

            def qk_split_hi(w, g, n, first=False):
                if not first and w == 0:
                    for s in (2 * g % SLOTS, 2 * g % SLOTS + 1):
                        act.wait_ge(s_stack[s], 192 * (2 * n + g // 2))
                act.wait_ge(s_qk, 8 * n + 2 * g + w + 1)
                act.activation(qk_hi[:, g % 2, w, :], mm_bank[w][:], ACT.Copy).then_inc(s_qkhi, 1)

            def side(kind, i, n):
                if kind in "WXH":
                    turned_hi("WXH".index(kind) * NT + i, n)
                elif kind == "V":
                    act.wait_ge(s_v, NT * n + i + 1)
                    act.activation(v_aug[:, i, :, 0:D], mm_bank[i % 2][:].rearrange("p (h d) -> p h d", h=H),
                                   ACT.Copy).then_inc(s_vcopy, 1)
                elif kind in "qkQK":
                    qk_split_hi(0 if kind in "qQ" else 1, i, n)

            def negate_max(n, u):
                s = u % SLOTS
                act.wait_ge(s_mt, 8 * n + u + 1)
                act.activation(neg_max[:], turned_max, ACT.Copy, scale=-1.0).then_inc(s_neg, 1)
                act.wait_ge(s_neg, 8 * n + u + 1)
                act.dma_start(q_stack[96:97, s, :, :].rearrange("p j (i t) -> p (j i) t", i=NT).bitcast(FP32),
                              neg_max[:].bitcast(FP32)).then_inc(s_negrow[s], 16)

            def copy_values(b, u):
                act.wait_ge(s_pv, 8 * b + u + 1)
                act.activation(values[0:PV_ROWS, :], pv_bank[0:PV_ROWS, :], ACT.Copy).then_inc(s_pvcopy, 1)

            def exponentials(b, u, j, k):
                act.wait_ge(s_st, 48 * b + 6 * u + 3 * j + k + 1)
                act.activation(prob[j][:, UNIT_COL[k]:UNIT_COL[k] + UNIT_LEN[k]],
                               exp_bank[(3 * j + k) % 2][:, 0:UNIT_LEN[k]], ACT.Exp, scale=SCALE).then_inc(s_exp, 1)

            for k in range(NK):
                act.wait_ge(s_wscaled, k + 1)
                raw = work[:, NF * (k % 3):NF * (k % 3) + NF]
                act.activation(w_hi[:, k, 0:2 * C].rearrange("p (h e) -> p h e", e=D)[:, :, 0:DS],
                               raw[:, 0:2 * H * DS].rearrange("p (h e) -> p h e", e=DS), ACT.Copy)
                act.activation(w_hi[:, k, 0:2 * C].rearrange("p (h e) -> p h e", e=D)[:, :, DS:D],
                               tails.rearrange("p q h e -> p (q h) e"), ACT.Copy)
                act.activation(w_hi[:, k, 2 * C:NF], raw[:, 2 * H * DS:2 * H * DS + C], ACT.Copy).then_inc(s_whi, 1)
                turned_hi(k, 0)
            for k in range(4, 8):
                turned_hi(k, 0)
            act.wait_ge(s_wload[NK], 16)
            act.activation(wp_hi[:], work[:, NF:NF + NK * C].rearrange("p (k c) -> p k c", k=NK),
                           ACT.Copy).then_inc(s_whi, 1)
            for k in range(8, 12):
                turned_hi(k, 0)
            for g in range(2):
                qk_split_hi(0, g, 0, first=True)
                qk_split_hi(1, g, 0, first=True)
            for i in range(NT):
                side("V", i, 0)
            negate_max(0, 0)

            def body(b, more):
                def fill(u, gap):
                    for kind, i in pieces(FILL[u][gap], more):
                        side(kind, i, b if kind in "VQK" else b + 1)

                def exp_pair(u, pair):
                    for unit in (2 * pair, 2 * pair + 1):
                        exponentials(b, u, unit // 3, unit % 3)

                def y_hi(i):
                    act.wait_ge(s_yt, NT * b + i + 1)
                    act.activation(wt_hi[:, :, P * i:P * i + P], y_bank[i][:].rearrange("p (k c) -> p k c", k=NK),
                                   ACT.Copy).then_inc(s_yhi, 1)

                for u in range(STEPS):
                    if u:
                        copy_values(b, u - 1)
                    for pair in range(3):
                        exp_pair(u, pair)
                        fill(u, pair)
                    if u + 1 < STEPS:
                        negate_max(b, u + 1)
                    fill(u, 3)
                copy_values(b, STEPS - 1)
                if more:
                    side("V", 0, b + 1)
                    side("V", 1, b + 1)
                for i in range(3):
                    y_hi(i)
                if more:
                    side("V", 2, b + 1)
                    side("V", 3, b + 1)
                y_hi(3)
                if more:
                    negate_max(b + 1, 0)

            per_batch(act, body)

        @block.vector
        def _(dve):
            chain = Chain(dve, s_dve)

            def x_tile(n, i):
                return x_all[:, n % 2, i, :] if isinstance(n, int) else x_all[:, bass.ds(n % 2, 1), i, :]

            def like_x(ap, n):
                return ap if isinstance(n, int) else ap.unsqueeze(1)

            def ctx_maxima(n):
                for i in range(NT):
                    dve.wait_ge(s_ctxload[i], 16 * n + 16)
                    last = dve.tensor_reduce(w_amax[:, NK * i:NK * i + NK],
                                             ctx_raw[:, i, :].rearrange("p (k c) -> p k c", k=NK),
                                             AX.X, ALU.max, apply_absolute_value=True)
                last.then_inc(s_amax, 1)

            def scales(amax, up, down, eps):
                chain(dve.tensor_scalar(down, amax, eps, None, ALU.max))
                chain(dve.reciprocal(up, down))
                dve.tensor_scalar(up, up, FP8_MAX, None, ALU.mult)
                return dve.tensor_scalar(down, down, 1.0 / FP8_MAX, None, ALU.mult)

            def ctx_scales(n):
                dve.wait_ge(s_top, n + 1)
                scales(w_top[:], w_up[:], w_down[:], W_EPS).then_inc(s_wscale, 1)

            def x_stats(n):
                for i in range(NT):
                    wait_apart(dve, s_xload[i], 16 * n + 16)
                    last = dve.bn_stats(bn1[:, i, :], x_tile(n, i))
                chain(last, wait_apart)
                for i in range(NT):
                    last = dve.bn_aggr(mv1[:, i, :], bn1[:, i, :])
                last.then_inc(s_var1, 1)

            def layernorm_x(n, i):
                k = NT + i
                if i == 0:
                    dve.wait_ge(s_rstd1, n + 1)
                dve.wait_ge(s_turn, 12 * n + i + 1)
                buf = tile_buf[:, k % 4, :]
                chain(dve.tensor_scalar(like_x(buf, n), x_tile(n, i), mv1[:, i, 0:1], rstd1[:, i:i + 1],
                                        ALU.subtract, ALU.mult))
                chain(dve.tensor_reduce(x_amax[:, i, :], buf.rearrange("p (k c) -> p k c", k=NK),
                                        AX.X, ALU.max, apply_absolute_value=True))
                scales(x_amax[:, i, :], x_up[:, i, :], x_down[:, i, :], ACT_EPS).then_inc(s_xscale, 1)

            def rounding(n, k):
                dve.wait_ge(s_scaled, 8 * n + k + 1)
                m = magic(n, k)
                chain(dve.tensor_scalar(m.bitcast(U16), tile_buf[:, k % 4, :].bitcast(U16)[:, 1::2],
                                        EXPONENT_BITS, None, ALU.bitwise_and))
                dve.tensor_scalar(m, m, MIN_NORMAL, MAGIC, ALU.max, ALU.mult).then_inc(s_magic, 1)

            def turned_lo(k, n):
                dve.wait_ge(s_thi, 12 * n + k + 1)
                hi, lo = (wt_hi, wt_lo) if k < NT else (xt_hi, xt_lo)
                cols = slice(P * (k % 4), P * (k % 4) + P)
                dve.tensor_tensor(lo[:, :, cols], turn_bank[:].rearrange("p (k c) -> p k c", k=NK),
                                  hi[:, :, cols].bitcast(FP32), ALU.subtract).then_inc(s_tlo, 1)

            def residual(n, i):
                dve.wait_ge(s_cross, NT * n + i + 1)
                chain(dve.scalar_tensor_tensor(x_tile(n, i), like_x(mm_bank[i % 2][:], n), gates[:, 0:1],
                                               x_tile(n, i), ALU.mult, ALU.add), wait_apart)
                chain(dve.bn_stats(bn2[:, i, :], x_tile(n, i)), wait_apart)
                dve.bn_aggr(mv2[:, i, :], bn2[:, i, :]).then_inc(s_x1, 1)

            def layernorm_x1(n, i):
                if i % 2 == 0:
                    dve.wait_ge(s_rstd2, 2 * n + i // 2 + 1)
                dve.wait_ge(s_turn, 12 * n + NT + i + 1)
                dve.tensor_scalar(like_x(tile_buf[:, i, :], n), x_tile(n, i), mv2[:, i, 0:1],
                                  rstd2[:, i:i + 1], ALU.subtract, ALU.mult).then_inc(s_hn, 1)

            def qk_split_lo(w, g, n):
                dve.wait_ge(s_qkhi, 8 * n + 2 * g + w + 1)
                dve.tensor_tensor(qk_lo[:, g % 2, w, :], mm_bank[w][:], qk_hi[:, g % 2, w, :].bitcast(FP32),
                                  ALU.subtract).then_inc(s_qklo, 1)

            def side(kind, i, n):
                if kind in "WXH":
                    turned_lo("WXH".index(kind) * NT + i, n)
                elif kind == "S":
                    residual(n, i)
                elif kind in "qkQK":
                    qk_split_lo(0 if kind in "qQ" else 1, i, n)

            def maxima(n, u, j, k):
                unit = 3 * j + k
                dve.wait_ge(s_sm, 48 * n + 6 * u + unit + 1)
                for i, col in MAX_UNITS[k]:
                    last = dve.tensor_reduce(row_max[:, NT * j + i:NT * j + i + 1],
                                             max_bank[unit % 2][:, col:col + P * (i + 1)], AX.X, ALU.max)
                last.then_inc(s_max, 1)

            def normalise(b, u):
                dve.wait_ge(s_pvt, 8 * b + u + 1)
                pv = pv_bank[:].rearrange("p (i j e) -> p j i e", j=2, i=NT)
                rd = rden[:].rearrange("p (j i) -> p j i", j=2)
                chain(dve.reciprocal(rd, pv[:, :, :, D]))
                dve.tensor_tensor(y[:, :, 2 * D * u:2 * D * u + 2 * D].rearrange("p i (j d) -> p j i d", j=2),
                                  pv[:, :, :, 0:D], rd.unsqueeze(3).broadcast_to([P, 2, NT, D]),
                                  ALU.mult).then_inc(s_norm, 1)

            def weight_chunk(k):
                raw = work[:, NF * (k % 3):NF * (k % 3) + NF]
                dve.wait_ge(s_wload[k], 16)
                std = raw[:, 0:2 * H * DS].rearrange("p (q h e) -> p q h e", q=2, h=H)
                v0 = 2 * H * DS
                low = raw[:, v0 + C:NF].rearrange("p (q h e) -> p q h e", q=2, h=H)
                for q in range(2):
                    dve.tensor_tensor(std[:, q], std[:, q],
                                      wsr_root[:, 0, :].unsqueeze(2).broadcast_to([P, H, DS]), ALU.mult)
                    last = dve.tensor_tensor(low[:, q], low[:, q],
                                             wsr_root[:, 1, :].unsqueeze(2).broadcast_to([P, H, R]), ALU.mult)
                chain(last)
                if k:
                    dve.wait_ge(s_whi, k)
                chain(dve.tensor_copy(tails, low))
                dve.copy_predicated(tails[:, 0], swap, low[:, 1])
                dve.copy_predicated(tails[:, 1], swap, low[:, 0]).then_inc(s_wscaled, 1)
                dve.wait_ge(s_whi, k + 1)
                hi = w_hi[:, k, :].bitcast(FP32)
                qk = w_lo[:, k, 0:2 * C].rearrange("p (h e) -> p h e", e=D)
                qk_h = hi[:, 0:2 * C].rearrange("p (h e) -> p h e", e=D)
                dve.tensor_tensor(qk[:, :, 0:DS], raw[:, 0:v0].rearrange("p (h e) -> p h e", e=DS),
                                  qk_h[:, :, 0:DS], ALU.subtract)
                dve.tensor_tensor(qk[:, :, DS:D], tails.rearrange("p q h e -> p (q h) e"),
                                  qk_h[:, :, DS:D], ALU.subtract)
                dve.tensor_tensor(w_lo[:, k, 2 * C:NF], raw[:, v0:v0 + C], hi[:, 2 * C:NF],
                                  ALU.subtract).then_inc(s_wlo, 1)

            dve.memset(pv_bank[:], 0.0).then_inc(s_cleared, 1)
            x_stats(0)
            ctx_maxima(0)
            dve.wait_ge(s_root, 1)
            chain(dve.tensor_scalar(swap, wsr[:, 1, :].unsqueeze(2).broadcast_to([P, H, R]), 0.1, None, ALU.is_gt))
            ctx_scales(0)
            rounding(0, 0)
            rounding(0, 1)
            weight_chunk(0)
            turned_lo(0, 0)
            rounding(0, 2)
            weight_chunk(1)
            turned_lo(1, 0)
            layernorm_x(0, 0)
            rounding(0, 3)
            weight_chunk(2)
            turned_lo(2, 0)
            layernorm_x(0, 1)
            rounding(0, 4)
            weight_chunk(3)
            turned_lo(3, 0)
            layernorm_x(0, 2)
            rounding(0, 5)
            turned_lo(4, 0)
            layernorm_x(0, 3)
            rounding(0, 6)
            turned_lo(5, 0)
            rounding(0, 7)
            turned_lo(6, 0)
            turned_lo(7, 0)
            dve.wait_ge(s_whi, NK + 1)
            dve.tensor_tensor(wp_lo[:], work[:, NF:NF + NK * C].rearrange("p (k c) -> p k c", k=NK),
                              wp_hi[:].bitcast(FP32), ALU.subtract).then_inc(s_wlo, 1)
            dve.wait_ge(s_tanh, 1)
            for i in range(NT):
                residual(0, i)
            for i in range(NT):
                layernorm_x1(0, i)
                turned_lo(8 + i, 0)
            for g in range(2):
                qk_split_lo(0, g, 0)
                qk_split_lo(1, g, 0)
            for unit in range(6):
                maxima(0, 0, unit // 3, unit % 3)
            first = chain.n
            dve.sem_inc(s_outt, FIRST_OUT)

            own = {(0, 0): [(ctx_scales, ())],
                   (0, 1): [(rounding, (0,))], (0, 2): [(x_stats, ())], (0, 3): [(rounding, (1,))],
                   (1, 0): [(rounding, (2,))], (1, 2): [(rounding, (3,)), (layernorm_x, (0,))],
                   (1, 3): [(layernorm_x, (1,))],
                   (2, 0): [(rounding, (4,))], (2, 1): [(rounding, (5,))], (2, 2): [(layernorm_x, (2,))],
                   (2, 3): [(layernorm_x, (3,))],
                   (3, 0): [(rounding, (6,))], (3, 2): [(rounding, (7,))],
                   (5, 0): [(layernorm_x1, (0,)), (layernorm_x1, (1,))],
                   (5, 3): [(layernorm_x1, (2,)), (layernorm_x1, (3,))]}

            def body(b, more):
                n = b + 1
                chain.at(first + DVE_CHAIN * b)

                def fill(u, gap):
                    for kind, i in pieces(FILL[u][gap], more):
                        side(kind, i, b if kind in "VQK" else n)
                    for f, a in own.get((u, gap), []) if more else []:
                        f(n, *a)

                def max_pair(n, u, pair):
                    for unit in (2 * pair, 2 * pair + 1):
                        maxima(n, u, unit // 3, unit % 3)

                for u in range(STEPS):
                    if u + 1 < STEPS:
                        max_pair(b, u + 1, 0)
                    if more and u == 0:
                        ctx_maxima(n)
                    for gap in range(4):
                        if u + 1 < STEPS and gap < 2:
                            max_pair(b, u + 1, gap + 1)
                        fill(u, gap)
                        if u and gap == 0:
                            normalise(b, u - 1)
                normalise(b, STEPS - 1)

                def y_lo(i):
                    dve.wait_ge(s_yhi, NT * b + i + 1)
                    dve.tensor_tensor(wt_lo[:, :, P * i:P * i + P], y_bank[i][:].rearrange("p (k c) -> p k c", k=NK),
                                      wt_hi[:, :, P * i:P * i + P].bitcast(FP32), ALU.subtract).then_inc(s_ylo, 1)

                for i in range(3):
                    y_lo(i)
                if more:
                    for pair in range(3):
                        max_pair(n, 0, pair)
                y_lo(3)
                for i in range(NT):
                    dve.wait_ge(s_wpmm, NT * b + i + 1)
                    dve.scalar_tensor_tensor(x_tile(b, i), like_x(mm_bank[i % 2][:], b), gates[:, 1:2],
                                             x_tile(b, i), ALU.mult, ALU.add).then_inc(s_outt, 1)
                if more:
                    assert chain.n == DVE_CHAIN, chain.n

            per_batch(dve, body)


_INS = ["x", "ctx_2048", "g_xattn", "g_ffn", "L0_ffn_Wa", "L0_ffn_Wp", "L0_ffn_w_std", "L0_ffn_w_rec"]


def kernel(**inputs):
    import numpy as np
    import concourse.bacc as bacc
    from concourse.bass_utils import run_bass_kernel_spmd

    nc = bacc.Bacc("TRN2", target_bir_lowering=False, num_devices=1)
    arrays, args = {}, []
    for name in _INS:
        a = np.ascontiguousarray(inputs[name])
        arrays[f"in_{name}"] = a
        args.append(nc.dram_tensor(f"in_{name}", a.shape, mybir.dt.from_np(a.dtype), kind="ExternalInput").ap())
    out = nc.dram_tensor("out", (B, T, C), FP32, kind="ExternalOutput").ap()
    flamingo_block(nc, *args, out)
    r = run_bass_kernel_spmd(nc, [arrays], core_ids=[0])
    return r.results[0]["out"]
```

```python
import concourse.bass as bass
from concourse import mybir
from concourse.alu_op_type import AluOpType as ALU
from contextlib import ExitStack

FP32 = mybir.dt.float32
FP32R = mybir.dt.float32r
BF16 = mybir.dt.bfloat16
U16 = mybir.dt.uint16
U32 = mybir.dt.uint32
ACT = mybir.ActivationFunctionType
AX = mybir.AxisListType

B, T, C = 4, 512, 512
H, D, R = 16, 32, 8
DS = D - R
P = 128
PV_ROWS = 64 + D + 1
NT = T // P
NK = C // P
NF = 3 * C
STEPS = H // 2
SLOTS = 4
SCALE = float(D) ** -0.5
FP8_MAX, ACT_EPS, W_EPS, LN_EPS = 448.0, 1e-4, 1e-6, 1e-5
MAGIC, MIN_NORMAL, EXPONENT_BITS = 1.5 * 2.0 ** 20, 2.0 ** -6, 0x7F80

MAX_UNITS = [[(3, 0)], [(2, 0), (0, 384)], [(1, 0)]]
EXP_UNITS = [[(0, 0)], [(1, 0), (3, 384)], [(2, 0)]]
PROB_COL = [0, 512, 1024, 896]
UNIT_COL = [0, 512, 1024]
UNIT_LEN = [512, 512, 256]

FILL = [
    ["Q2", "", "", "K2"],
    ["Q3", "W0", "", "W1"],
    ["K3", "W2", "", "W3"],
    ["X0", "X1", "S0", ""],
    ["S1 X2", "X3", "", "S2"],
    ["S3", "H0", "", "H1"],
    ["H2", "H3", "", "q0"],
    ["k0", "", "q1", "k1"],
]
LAST_FILL = [
    ["Q2", "", "", "K2"],
    ["Q3", "", "", ""],
    ["K3", "", "", "Y0"],
    ["Y1", "", "", ""],
    ["Y2", "", "", "Y3"],
    ["Y4", "", "", ""],
    ["Y5", "", "", "Y6"],
    ["", "", "", "Y7"],
]
DOWN = {(1, 0): [0], (1, 2): [1], (2, 0): [2], (2, 2): [3],
        (2, 3): [4], (3, 0): [5], (3, 2): [6], (4, 0): [7]}
DVE_CHAIN, POOL_CHAIN = 43, 11


def pieces(u, gap, more):
    for name in (FILL if more else LAST_FILL)[u][gap].split():
        yield name[0], int(name[1])


class Chain:

    def __init__(self, eng, sem):
        self.eng, self.sem, self.base, self.n = eng, sem, 0, 0

    def __call__(self, ins, wait=lambda eng, sem, count: eng.wait_ge(sem, count)):
        self.n += 1
        ins.then_inc(self.sem, 1)
        wait(self.eng, self.sem, self.base + self.n)

    def at(self, base):
        self.base, self.n = base, 0


def flamingo_block(nc, x, ctx, g_xattn, g_ffn, wa, wp, w_std, w_rec, out):
    es = ExitStack()
    with es:
        def sb(name, shape, dt=FP32):
            return es.enter_context(nc.sbuf_tensor(name, shape, dt))

        def pb(name, dt=FP32):
            return es.enter_context(nc.psum_tensor(name, [P, 512], dt))

        def sem(name):
            return es.enter_context(nc.semaphore(name))

        w_hi, w_lo = sb("w_hi", [P, NK, NF], FP32R), sb("w_lo", [P, NK, NF], FP32R)
        wp_hi, wp_lo = sb("wp_hi", [P, NK, C], FP32R), sb("wp_lo", [P, NK, C], FP32R)
        q_stack = sb("q_stack", [97, SLOTS, 2, T], FP32R)
        k_stack = sb("k_stack", [97, SLOTS, 2, T], FP32R)
        qk_hi = sb("qk_hi", [P, 2, 2, T], FP32R)
        qk_lo = sb("qk_lo", [P, 2, 2, T], FP32R)
        xt_hi, xt_lo = sb("xt_hi", [P, NK, T], FP32R), sb("xt_lo", [P, NK, T], FP32R)
        wt_hi, wt_lo = sb("wt_hi", [P, NK, T], FP32R), sb("wt_lo", [P, NK, T], FP32R)
        x_all = sb("x_all", [P, 2, NT, C])
        ctx_raw = sb("ctx_raw", [P, NT, C])
        tile_buf = sb("tile_buf", [P, 4, C])
        v_aug = sb("v_aug", [P, NT, H, D + 1])
        work = sb("work", [P, 4608])
        prob = [work[:, 0:1280], work[:, 1280:2560]]
        y = work[:, 2560:4608].rearrange("p (i c) -> p i c", i=NT)
        values = sb("values", [P, T])

        def magic(n, k):
            if isinstance(n, int) and n == 0:
                place = (values if k < NT else x_all[:, 1, 2, :])[:, 256 * (k % 2):256 * (k % 2) + 256]
            else:
                place = y[:, k % 2, 256:512]
            return place.bitcast(BF16)

        ident = sb("ident", [P, P])
        ident_bf = sb("ident_bf", [P, P], BF16)
        future = sb("future", [P, P], BF16)
        gates = sb("gates", [P, 2])
        wsr = sb("wsr", [P, 2, H])
        root_col = sb("root_col", [2 * H, 1])
        wsr_root = sb("wsr_root", [P, 2, H])
        neg_half = sb("neg_half", [P, NT])
        spare = x_all[:, 1, 0, :]
        swap = spare[:, 256:256 + H * R].bitcast(U32).rearrange("p (h e) -> p h e", h=H)
        half = spare[0:2 * H, 384:385]
        ones = spare[0:2 * H, 0:P]
        root_diag = spare[0:2 * H, P:P + 2 * H]
        tails = [x_all[:, 1, 1 + 2 * (i // 2), 256 * (i % 2):256 * (i % 2) + 2 * H * R]
                 .rearrange("p (q h e) -> p q h e", q=2, h=H) for i in range(NK)]
        late_raw = qk_hi[:].bitcast(FP32).rearrange("p g w t -> p (g w t)")[:, 0:NF]
        raw_w = [work[:, 0:NF], work[:, NF:2 * NF], work[:, 2 * NF:3 * NF], late_raw]
        raw_wp = y[:]
        first_x = qk_lo[:].bitcast(FP32).rearrange("p g w t -> p (g w) t")
        w_amax, w_top = sb("w_amax", [P, NT * NK]), sb("w_top", [P, NT * NK])
        w_up, w_down = sb("w_up", [P, NT * NK]), sb("w_down", [P, NT * NK])
        x_amax = sb("x_amax", [P, NT, NK])
        x_up, x_down = sb("x_up", [P, NT, NK]), sb("x_down", [P, NT, NK])
        bn1, mv1 = sb("bn1", [P, NT, 6]), sb("mv1", [P, NT, 2])
        bn2, mv2 = sb("bn2", [P, NT, 6]), sb("mv2", [P, NT, 2])
        rstd1, rstd2 = sb("rstd1", [P, NT]), sb("rstd2", [P, NT])
        row_max = sb("row_max", [P, 2, 8])
        neg_max = sb("neg_max", [8, P], FP32R)
        rden = sb("rden", [P, 8])

        max_bank = [pb("max_bank0"), pb("max_bank1")]
        exp_bank = [pb("exp_bank0"), pb("exp_bank1")]
        pv_bank = pb("pv_bank")
        turn_bank = pb("turn_bank")
        turned_max = exp_bank[0][0:8, 0:P]
        mm_bank = [pb("mm_bank0"), pb("mm_bank1")]
        y_bank = [exp_bank[0], exp_bank[1], turn_bank, exp_bank[1]]

        s_begun = sem("s_begun")
        s_const = sem("s_const")
        s_cleared = sem("s_cleared")
        s_small = sem("s_small")
        s_tanh = sem("s_tanh")
        s_root = sem("s_root")
        s_diag, s_spread = sem("s_diag"), sem("s_spread")
        s_wload = [sem(f"s_wload{i}") for i in range(NK + 1)]
        s_wscaled = sem("s_wscaled")
        s_whi = sem("s_whi")
        s_wlo = sem("s_wlo")
        s_wvlo = sem("s_wvlo")
        s_xround = sem("s_xround")
        s_xload = [sem(f"s_xload{i}") for i in range(NT)]
        s_ctxload = [sem(f"s_ctxload{i}") for i in range(NT)]
        s_amax = sem("s_amax")
        s_top = sem("s_top")
        s_wscale = sem("s_wscale")
        s_var1, s_rstd1 = sem("s_var1"), sem("s_rstd1")
        s_rstd2 = sem("s_rstd2")
        s_xscale = sem("s_xscale")
        s_scaled = sem("s_scaled")
        s_magic = sem("s_magic")
        s_round = sem("s_round")
        s_quant = sem("s_quant")
        s_hn = sem("s_hn")
        s_turn = sem("s_turn")
        s_thi, s_tlo = sem("s_thi"), sem("s_tlo")
        s_cross, s_x1 = sem("s_cross"), sem("s_x1")
        s_qk, s_qkhi, s_qklo = sem("s_qk"), sem("s_qkhi"), sem("s_qklo")
        s_v, s_vcopy = sem("s_v"), sem("s_vcopy")
        s_stack = [sem(f"s_stack{i}") for i in range(SLOTS)]
        s_negrow = [sem(f"s_negrow{i}") for i in range(SLOTS)]
        s_sm, s_max = sem("s_sm"), sem("s_max")
        s_mt, s_neg = sem("s_mt"), sem("s_neg")
        s_st, s_exp = sem("s_st"), sem("s_exp")
        s_causal = sem("s_causal")
        s_pv = sem("s_pv")
        s_pvcopy, s_pvt = sem("s_pvcopy"), sem("s_pvt")
        s_norm = sem("s_norm")
        s_yt, s_yhi, s_ylo = sem("s_yt"), sem("s_yhi"), sem("s_ylo")
        s_wpmm = sem("s_wpmm")
        s_outt = sem("s_outt")
        s_store = sem("s_store")
        s_dve = sem("s_dve")
        s_pool = sem("s_pool")

        FIRST_OUT = NT

        def wait_apart(eng, sem, count):
            if not isinstance(count, int):
                count = eng.to_reg(count)
                eng.wait_ge(s_begun, 1)
            eng.wait_ge(sem, count)

        def per_batch(eng, body, peeled=1):
            with eng.Fori(0, B - peeled) as b:
                body(b, True)
            for b in range(B - peeled, B):
                body(b, b < B - 1)

        def late_output(b):
            return isinstance(b, int) and b == B - 2

        FIRST_TURNS = [(name[0], int(name[1])) for name in "W0 X0 W1 W2 W3 X1 X2 X3 H0 H1 H2 H3".split()]

        def first_bank(p):
            return (turn_bank, exp_bank[0])[p % 2]

        block = es.enter_context(nc.Block())

        @block.sync
        def _(sp):
            x_v = x.rearrange("b (i p) c -> b i p c", p=P)
            ctx_v = ctx.rearrange("b (i p) c -> b i p c", p=P)
            out_v = out.rearrange("b (i p) c -> b i p c", p=P)

            def load_tiles(n, parity):
                for i in range(NT):
                    sp.dma_start(x_all[:, parity, i, :], x_v[n, i, :, :]).then_inc(s_xload[i], 16)

            def load_ctx(n):
                for i in range(NT):
                    if isinstance(n, int):
                        src, dst = ctx_v[n, i, :, :], ctx_raw[:, i, :]
                    else:
                        src = ctx_v[bass.ds(n, 1), i, :, :].rearrange("a p c -> p a c")
                        dst = ctx_raw[:, i:i + 1, :]
                    sp.dma_start(dst, src).then_inc(s_ctxload[i], 16)

            def stack(n, u, first=False):
                g, s = u // 2, u % SLOTS
                if not first:
                    wait_apart(sp, s_st, 48 * n + 6 * (u - SLOTS) + 6)
                for dst, w, parts in ((q_stack, 0, (qk_hi, qk_lo, qk_hi)), (k_stack, 1, (qk_hi, qk_hi, qk_lo))):
                    wait_apart(sp, s_qklo, 8 * n + 2 * g + w + 1)
                    for j in range(2):
                        rows = slice(D * (2 * (u % 2) + j), D * (2 * (u % 2) + j) + D)
                        for a, part in enumerate(parts):
                            sp.dma_start(dst[D * a:D * a + D, s, j, :].bitcast(FP32),
                                         part[rows, g % 2, w, :].bitcast(FP32)).then_inc(s_stack[s], 16)

            load_tiles(0, 0)
            load_ctx(0)
            wa_v = wa.rearrange("(k p) f -> p k f", p=P)
            for k in range(NK):
                sp.dma_start(raw_w[k], wa_v[:, k, :]).then_inc(s_wload[k], 16)
            sp.wait_ge(s_scaled, NT)
            load_ctx(1)
            sp.wait_ge(s_wvlo, NK)
            sp.dma_start(raw_wp, wp.rearrange("(k p) c -> p k c", p=P)).then_inc(s_wload[NK], 16)
            for u in range(SLOTS):
                stack(0, u, first=True)

            def body(b, more, ctx_more):
                if more:
                    for i in range(NT):
                        if isinstance(b, int):
                            dst, src = x_all[:, (b + 1) % 2, i, :], x_v[b + 1, i, :, :]
                        else:
                            dst = x_all[:, bass.ds((b + 1) % 2, 1), i, :]
                            src = x_v[bass.ds(b + 1, 1), i, :, :].rearrange("a p c -> p a c")
                        sp.dma_start(dst, src).then_inc(s_xload[i], 16)
                for u in range(SLOTS, STEPS):
                    stack(b, u)
                if ctx_more:
                    wait_apart(sp, s_scaled, 8 * b + 8 + NT)
                    load_ctx(b + 2)
                if more:
                    for u in range(SLOTS):
                        stack(b + 1, u)
                for done in () if late_output(b) else (B - 2, b) if isinstance(b, int) else (b,):
                    for i in range(NT):
                        wait_apart(sp, s_outt, FIRST_OUT + NT * done + i + 1)
                        if isinstance(done, int):
                            dst, src = out_v[done, i, :, :], x_all[:, done % 2, i, :]
                        else:
                            dst = out_v[bass.ds(done, 1), i, :, :].rearrange("a p c -> p a c")
                            src = x_all[:, bass.ds(done % 2, 1), i, :]
                        sp.dma_start(dst, src).then_inc(s_store, 16)
                if not late_output(b):
                    wait_apart(sp, s_store, 16 * NT * b + 16 * NT)

            with sp.Fori(0, B - 2) as b:
                body(b, True, True)
            body(B - 2, True, False)
            body(B - 1, False, False)

        @block.gpsimd
        def _(pool):
            chain = Chain(pool, s_pool)
            pool.memset(neg_half[:], -0.5).then_inc(s_begun, 1)
            chain(pool.memset(ident[:], 0.0))
            chain(pool.affine_select(out=ident[:], in_=ident[:], compare_op=ALU.not_equal, fill=1.0,
                                     base=0, pattern=[[-1, P]], channel_multiplier=1))
            pool.tensor_copy(ident_bf[:], ident[:]).then_inc(s_const, 1)
            chain(pool.memset(future[:], 0.0))
            pool.affine_select(out=future[:], in_=future[:], compare_op=ALU.is_ge, fill=-3.0e38,
                               base=0, pattern=[[-1, P]], channel_multiplier=1).then_inc(s_const, 1)
            pool.wait_ge(s_const, 2)
            pool.memset(k_stack[96:97, :, :, :].bitcast(FP32), 1.0).then_inc(s_const, 1)
            pool.wait_ge(s_const, 3)
            pool.memset(v_aug[:, :, :, D:D + 1], 1.0)
            pool.memset(half, 0.5)
            chain(pool.memset(ones, 1.0))

            def top(n):
                wait_apart(pool, s_amax, n + 1)
                pool.partition_all_reduce(w_top[:], w_amax[:], P, bass.bass_isa.ReduceOp.max).then_inc(s_top, 1)

            def inv_std(n, mv, rstd, lo, hi, var_sem, rstd_sem, count):
                wait_apart(pool, var_sem, count)
                chain(pool.tensor_scalar(rstd[:, lo:hi], mv[:, lo:hi, 1], LN_EPS, None, ALU.add))
                pool.tensor_tensor(rstd[:, lo:hi], rstd[:, lo:hi], neg_half[:, lo:hi], ALU.pow).then_inc(rstd_sem, 1)

            def inv_std1(n):
                inv_std(n, mv1, rstd1, 0, NT, s_var1, s_rstd1, n + 1)

            def inv_std2(n, pair):
                inv_std(n, mv2, rstd2, 2 * pair, 2 * pair + 2, s_x1, s_rstd2, NT * n + 2 * pair + 2)

            def blocks(ap):
                return ap.rearrange("p (k c) -> p k c", k=NK)

            def spread(scales):
                return scales.unsqueeze(2).broadcast_to([P, NK, P])

            def scale_up(n, k):
                buf = tile_buf[:, k % 4, :]
                if k < NT:
                    if k == 0:
                        pool.wait_ge(s_wscale, n + 1)
                    src, up = ctx_raw[:, k, :], w_up[:, NK * k:NK * k + NK]
                else:
                    pool.wait_ge(s_xscale, NT * n + k - NT + 1)
                    src, up = buf, x_up[:, k - NT, :]
                pool.tensor_tensor(blocks(buf), blocks(src), spread(up), ALU.mult).then_inc(s_scaled, 1)

            def quantise(n, k):
                buf = tile_buf[:, k % 4, :]
                pool.wait_ge(s_magic, 8 * n + k + 1)
                chain(pool.tensor_tensor(buf, buf, magic(n, k), ALU.add))
                pool.tensor_tensor(buf, buf, magic(n, k), ALU.subtract).then_inc(s_round, 1)

            def zero_future(b, u, j):
                wait_apart(pool, s_exp, 48 * b + 6 * u + 3 * j + 3)
                three = prob[j].rearrange("p (a c) -> p a c", c=256)[:, 0:5:2, 0:P]
                pool.affine_select(out=three, in_=three, compare_op=ALU.is_ge, fill=0.0,
                                   base=0, pattern=[[0, 3], [1, P]], channel_multiplier=-1)
                fourth = prob[j][:, PROB_COL[3]:PROB_COL[3] + P]
                last = pool.affine_select(out=fourth, in_=fourth, compare_op=ALU.is_ge, fill=0.0,
                                          base=0, pattern=[[1, P]], channel_multiplier=-1)
                if j:
                    last.then_inc(s_causal, 1)

            def weight_lo(k):
                raw, tail = raw_w[k], tails[k]
                v0 = 2 * H * DS
                pool.wait_ge(s_whi, k + 1)
                hi = w_hi[:, k, :].bitcast(FP32)
                qk = w_lo[:, k, 0:2 * C].rearrange("p (h e) -> p h e", e=D)
                qk_h = hi[:, 0:2 * C].rearrange("p (h e) -> p h e", e=D)
                pool.tensor_tensor(qk[:, :, 0:DS], raw[:, 0:v0].rearrange("p (h e) -> p h e", e=DS),
                                   qk_h[:, :, 0:DS], ALU.subtract)
                pool.tensor_tensor(qk[:, :, DS:D], tail.rearrange("p q h e -> p (q h) e"),
                                   qk_h[:, :, DS:D], ALU.subtract).then_inc(s_wlo, 1)

            def weight_lo_v(k):
                v0 = 2 * H * DS
                pool.tensor_tensor(w_lo[:, k, 2 * C:NF], raw_w[k][:, v0:v0 + C],
                                   w_hi[:, k, 2 * C:NF].bitcast(FP32), ALU.subtract).then_inc(s_wvlo, 1)

            def first_scale_up(i):
                pool.wait_ge(s_xscale, i)
                buf = blocks(first_x[:, i, :])
                pool.tensor_tensor(buf, buf, spread(x_up[:, i, :]), ALU.mult).then_inc(s_scaled, 1)

            def first_round(i):
                buf = first_x[:, i, :]
                pool.wait_ge(s_magic, NT + i)
                chain(pool.tensor_tensor(buf, buf, magic(0, NT + i), ALU.add))
                pool.tensor_tensor(buf, buf, magic(0, NT + i), ALU.subtract).then_inc(s_round, 1)

            inv_std1(0)
            pool.wait_ge(s_small, 96)
            chain(pool.tensor_scalar(root_col[:], root_col[:], 1e-8, None, ALU.max))
            pool.tensor_tensor(root_col[:], root_col[:], half, ALU.pow).then_inc(s_root, 1)
            top(0)
            scale_up(0, 0)
            scale_up(0, 1)
            for k in range(NT):
                quantise(0, k)
                if k + 2 < NT:
                    scale_up(0, k + 2)
            first_scale_up(1)
            first_scale_up(2)
            first_round(1)
            first_scale_up(3)
            first_round(2)
            first_round(3)
            weight_lo(0)
            weight_lo(1)
            inv_std2(0, 0)
            weight_lo(2)
            inv_std2(0, 1)
            weight_lo(3)
            for k in (3, 0, 1, 2):
                weight_lo_v(k)
            pool.wait_ge(s_whi, NK + 1)
            pool.tensor_tensor(wp_lo[:], raw_wp, wp_hi[:].bitcast(FP32), ALU.subtract).then_inc(s_wvlo, 1)
            pool.sem_inc(s_scaled, 1)
            pool.sem_inc(s_round, 1)
            first = chain.n

            def body(b, more):
                n = b + 1
                chain.at(first + POOL_CHAIN * b)
                before = {0: [(top, []), (scale_up, [0]), (scale_up, [1])],
                          1: [(inv_std1, []), (scale_up, [3]), (quantise, [2])],
                          2: [(quantise, [4]), (scale_up, [5])],
                          3: [(scale_up, [7]), (quantise, [6])],
                          4: [(inv_std2, [0])],
                          5: [(inv_std2, [1])]}
                after = {0: [(quantise, [0]), (scale_up, [2]), (quantise, [1])],
                         1: [(quantise, [3]), (scale_up, [4])],
                         2: [(quantise, [5]), (scale_up, [6])],
                         3: [(quantise, [7])]}
                for u in range(STEPS):
                    for f, a in before.get(u, []) if more else []:
                        f(n, *a)
                    zero_future(b, u, 0)
                    zero_future(b, u, 1)
                    for f, a in after.get(u, []) if more else []:
                        f(n, *a)
                if more:
                    assert chain.n == POOL_CHAIN, chain.n

            per_batch(pool, body)

        @block.tensor
        def _(pe):
            def split_product(dst, l_hi, l_lo, r_hi, r_lo, done):
                for k in range(NK):
                    pe.matmul(dst, l_hi(k), r_hi(k), start=(k == 0), stop=False)
                    pe.matmul(dst, l_hi(k), r_lo(k), start=False, stop=False)
                    last = pe.matmul(dst, l_lo(k), r_hi(k), start=False, stop=(k == NK - 1))
                last.then_inc(done, 1)

            def turn(src, done, bank=turn_bank):
                for k in range(NK):
                    last = pe.transpose(bank[:, P * k:P * k + P], src[:, P * k:P * k + P], ident[:])
                last.then_inc(done, 1)

            def rows_of(t, i):
                return lambda k: t[:, k, P * i:P * i + P]

            def cols_of(t, lo, n):
                return lambda k: t[:, k, lo:lo + n]

            def side(kind, i, n, more, first=False):
                if kind in "WX":
                    k = i + (NT if kind == "X" else 0)
                    pe.wait_ge(s_quant, 8 * n + k + 1)
                    if k:
                        pe.wait_ge(s_tlo, 12 * n + k)
                    turn(tile_buf[:, k % 4, :], s_turn)
                elif kind == "H":
                    pe.wait_ge(s_hn, NT * n + i + 1)
                    pe.wait_ge(s_tlo, 12 * n + 8 + i)
                    turn(tile_buf[:, i % 4, :], s_turn)
                elif kind == "S":
                    if i >= 2:
                        pe.wait_ge(s_x1, NT * n + i - 1)
                    elif not first:
                        pe.wait_ge(s_qklo, 8 * n - 1 + i)
                    pe.wait_ge(s_tlo, NT + 1 + i if first else 12 * n + NT + i + 1)
                    split_product(mm_bank[i % 2][:], rows_of(xt_hi, i), rows_of(xt_lo, i),
                                  cols_of(wt_hi, 0, C), cols_of(wt_lo, 0, C), s_cross)
                elif kind == "V":
                    if i < 2:
                        pe.wait_ge(s_qklo, 1 + i if first else 8 * n + 3 + i)
                    else:
                        pe.wait_ge(s_vcopy, NT * n + i - 1)
                    split_product(mm_bank[i % 2][:], rows_of(xt_hi, i), rows_of(xt_lo, i),
                                  cols_of(w_hi, 2 * C, C), cols_of(w_lo, 2 * C, C), s_v)
                else:
                    w, g = (0 if kind in "qQ" else 1), i
                    if g == 0:
                        pe.wait_ge(s_x1, NT * n + 3 + w)
                    elif g == 2:
                        pe.wait_ge(s_vcopy, NT * n + 3 + w)
                        pe.wait_ge(s_qklo, 8 * n + 3 + w)
                        if more:
                            pe.wait_ge(s_outt, FIRST_OUT + NT * n - 1 + w)
                    else:
                        pe.wait_ge(s_qklo, 8 * n + 2 * g - 1 + w)
                    if g == 0:
                        pe.wait_ge(s_tlo, 12 * n + 12)
                    at = C * w + P * g
                    split_product(mm_bank[w][:], cols_of(w_hi, at, P), cols_of(w_lo, at, P),
                                  cols_of(xt_hi, 0, T), cols_of(xt_lo, 0, T), s_qk)

            def scores_for_max(n, u, j, k, first=False):
                s, unit = u % SLOTS, 3 * j + k
                if unit == 0:
                    pe.wait_ge(s_stack[s], 192 * (2 * n + u // SLOTS + 1))
                if unit >= 2 or not first:
                    pe.wait_ge(s_max, 48 * n + 6 * u + unit - 1)
                bank = max_bank[unit % 2]
                for i, col in MAX_UNITS[k]:
                    width = P * (i + 1)
                    pe.matmul(bank[:, col:col + width], q_stack[0:96, s, j, P * i:P * i + P],
                              k_stack[0:96, s, j, 0:width], start=True, stop=False)
                    last = pe.matmul(bank[:, col + P * i:col + width], ident_bf[:], future[:],
                                     start=False, stop=True)
                last.then_inc(s_sm, 1)

            def transpose_max(n, u):
                pe.wait_ge(s_max, 48 * n + 6 * u + 6)
                pe.transpose(turned_max, row_max[:, u % 2, :], ident[:]).then_inc(s_mt, 1)

            def scores_t(b, u, j, k):
                s, unit = u % SLOTS, 3 * j + k
                if unit == 0:
                    pe.wait_ge(s_negrow[s], 16 * (2 * b + u // SLOTS + 1))
                if unit >= 2:
                    pe.wait_ge(s_exp, 48 * b + 6 * u + unit - 1)
                bank = exp_bank[unit % 2]
                for i, col in EXP_UNITS[k]:
                    last = pe.matmul(bank[:, col:col + T - P * i], k_stack[0:97, s, j, P * i:P * i + P],
                                     q_stack[0:97, s, j, P * i:T], start=True, stop=True)
                last.then_inc(s_st, 1)

            def weighted_values(b, u):
                if u == 0:
                    pe.wait_ge(s_vcopy, NT * b + NT)
                else:
                    pe.wait_ge(s_norm, 8 * b + u)
                pe.wait_ge(s_causal, 8 * b + u + 1)
                for m in range(NT):
                    for j in range(2):
                        last = pe.matmul(pv_bank[64 * j:64 * j + D + 1, P * m:T], v_aug[:, m, 2 * u + j, :],
                                         prob[j][:, PROB_COL[m]:PROB_COL[m] + T - P * m],
                                         start=(m == 0), stop=(m == NT - 1))
                last.then_inc(s_pv, 1)

            def turn_values(b, u):
                pe.wait_ge(s_pvcopy, 8 * b + u + 1)
                for i in range(NT):
                    last = pe.transpose(pv_bank[:, P * i:P * i + PV_ROWS], values[0:PV_ROWS, P * i:P * i + P],
                                        ident[0:PV_ROWS, 0:PV_ROWS])
                last.then_inc(s_pvt, 1)

            def turn_y(b, i):
                if i == 0:
                    pe.wait_ge(s_norm, 8 * b + 8)
                if i == 3:
                    pe.wait_ge(s_ylo, NT * b + 2)
                turn(y[:, i, :], s_yt, y_bank[i])

            def out_half(b, half):
                i, second = half // 2, half % 2
                bank = mm_bank[i % 2][:]
                if not second:
                    pe.wait_ge(s_ylo, NT * b + i + 1)
                for k in (2, 3) if second else (0, 1):
                    y_h, y_l = wt_hi[:, k, P * i:P * i + P], wt_lo[:, k, P * i:P * i + P]
                    pe.matmul(bank, y_h, wp_hi[:, k, :], start=(k == 0), stop=False)
                    pe.matmul(bank, y_h, wp_lo[:, k, :], start=False, stop=False)
                    last = pe.matmul(bank, y_l, wp_hi[:, k, :], start=False, stop=(k == NK - 1))
                if second:
                    last.then_inc(s_wpmm, 1)

            def out_product(b, i, more):
                if i < 2 and more:
                    pe.wait_ge(s_vcopy, NT * b + NT + 3 + i)
                else:
                    pe.wait_ge(s_outt, FIRST_OUT + NT * b + i - 1)
                out_half(b, 2 * i)
                out_half(b, 2 * i + 1)

            def late_half(half):
                b, i = B - 2, half // 2
                if half % 2 == 0 and i < 2:
                    pe.wait_ge(s_qklo, 8 * (B - 1) + 7 + i)
                elif half % 2 == 0:
                    pe.wait_ge(s_outt, FIRST_OUT + NT * b + i - 1)
                out_half(b, half)

            pe.wait_ge(s_cleared, 1)
            pe.wait_ge(s_const, 1)
            pe.wait_ge(s_diag, 1)
            pe.matmul(exp_bank[1][:, 0:2 * H], ones, root_diag, start=True, stop=True).then_inc(s_spread, 1)
            for p, (kind, i) in enumerate(FIRST_TURNS):
                if kind in "WX":
                    pe.wait_ge(s_quant, p + 1)
                else:
                    pe.wait_ge(s_hn, i + 1)
                if p >= 2:
                    pe.wait_ge(s_tlo, p - 1)
                turn(first_x[:, i, :] if kind == "X" else tile_buf[:, i, :], s_turn, first_bank(p))
                for k in {5: (0,), 6: (1,), 7: (2, 3)}.get(p, ()):
                    side("S", k, 0, True, first=True)
            pe.wait_ge(s_tlo, 12)
            pe.wait_ge(s_wlo, NK)
            side("q", 0, 0, True)
            side("k", 0, 0, True)
            pe.wait_ge(s_wvlo, NK)
            for i in range(3):
                side("V", i, 0, True, first=True)
            pe.wait_ge(s_const, 3)
            for unit in (0, 1):
                scores_for_max(0, 0, 0, unit, first=True)
            pe.wait_ge(s_vcopy, NT - 1)
            side("q", 1, 0, True)
            for unit in (2, 3):
                scores_for_max(0, 0, unit // 3, unit % 3, first=True)
            side("V", 3, 0, True, first=True)
            for unit in (4, 5):
                scores_for_max(0, 0, 1, unit - 3, first=True)
            pe.wait_ge(s_vcopy, NT)
            side("k", 1, 0, True)
            pe.wait_ge(s_wvlo, NK + 1)

            def body(b, more):
                def fill(u, gap):
                    for kind, i in pieces(u, gap, more):
                        if kind == "Y":
                            late_half(i)
                        else:
                            side(kind, i, b if kind in "VQK" else b + 1, more)

                def max_pair(n, u, pair):
                    for unit in (2 * pair, 2 * pair + 1):
                        scores_for_max(n, u, unit // 3, unit % 3)

                def exp_pair(u, pair):
                    for unit in (2 * pair, 2 * pair + 1):
                        scores_t(b, u, unit // 3, unit % 3)

                for u in range(STEPS):
                    ahead = u + 1 < STEPS
                    if ahead:
                        max_pair(b, u + 1, 0)
                    if u:
                        pe.wait_ge(s_exp, 48 * b + 6 * u - 1)
                    transpose_max(b, u)
                    fill(u, 0)
                    if u:
                        weighted_values(b, u - 1)
                    if not (u or more):
                        pe.wait_ge(s_ylo, NT * b)
                    exp_pair(u, 0)
                    if ahead:
                        max_pair(b, u + 1, 1)
                    fill(u, 1)
                    if u:
                        turn_values(b, u - 1)
                    exp_pair(u, 1)
                    if ahead:
                        max_pair(b, u + 1, 2)
                    fill(u, 2)
                    exp_pair(u, 2)
                    fill(u, 3)
                n = b + 1
                if more:
                    side("V", 0, n, more)
                weighted_values(b, STEPS - 1)
                if more:
                    side("V", 1, n, more)
                turn_values(b, STEPS - 1)
                for i in range(3):
                    turn_y(b, i)
                if more:
                    max_pair(n, 0, 0)
                    side("V", 2, n, more)
                    max_pair(n, 0, 1)
                    side("V", 3, n, more)
                    max_pair(n, 0, 2)
                turn_y(b, 3)
                if not late_output(b):
                    for i in range(NT):
                        out_product(b, i, more)

            per_batch(pe, body, peeled=2)

        @block.scalar
        def _(act):
            act.dma_start(gates[:, 0:1], g_xattn.partition_broadcast(P)).then_inc(s_small, 16)
            act.dma_start(gates[:, 1:2], g_ffn.partition_broadcast(P)).then_inc(s_small, 16)
            act.dma_start(wsr[:, 0, :], w_std.partition_broadcast(P)).then_inc(s_small, 16)
            act.dma_start(wsr[:, 1, :], w_rec.partition_broadcast(P)).then_inc(s_small, 16)
            act.dma_start(root_col[0:H, :], w_std.rearrange("(h o) -> h o", o=1)).then_inc(s_small, 16)
            act.dma_start(root_col[H:2 * H, :], w_rec.rearrange("(h o) -> h o", o=1)).then_inc(s_small, 16)
            act.wait_ge(s_small, 96)
            act.activation(gates[:], gates[:], ACT.Tanh).then_inc(s_tanh, 1)

            def turned_hi(k, n):
                act.wait_ge(s_turn, 12 * n + k + 1)
                dst = (wt_hi if k < NT else xt_hi)[:, :, P * (k % 4):P * (k % 4) + P]
                act.activation(dst, turn_bank[:].rearrange("p (k c) -> p k c", k=NK), ACT.Copy).then_inc(s_thi, 1)

            def scale_down(n, k):
                act.wait_ge(s_round, 8 * n + k + 1)
                for j in range(NK):
                    down = w_down[:, NK * k + j:NK * k + j + 1] if k < NT else x_down[:, k - NT, j:j + 1]
                    part = tile_buf[:, k % 4, P * j:P * j + P]
                    last = act.activation(part, part, ACT.Copy, scale=down)
                last.then_inc(s_quant, 1)

            def qk_split_hi(w, g, n, first=False):
                if not first and w == 0:
                    for s in (2 * g % SLOTS, 2 * g % SLOTS + 1):
                        act.wait_ge(s_stack[s], 192 * (2 * n + g // 2))
                act.wait_ge(s_qk, 8 * n + 2 * g + w + 1)
                act.activation(qk_hi[:, g % 2, w, :], mm_bank[w][:], ACT.Copy).then_inc(s_qkhi, 1)

            def side(kind, i, n):
                if kind in "WXH":
                    turned_hi("WXH".index(kind) * NT + i, n)
                elif kind == "V":
                    act.wait_ge(s_v, NT * n + i + 1)
                    act.activation(v_aug[:, i, :, 0:D], mm_bank[i % 2][:].rearrange("p (h d) -> p h d", h=H),
                                   ACT.Copy).then_inc(s_vcopy, 1)
                elif kind in "qkQK":
                    qk_split_hi(0 if kind in "qQ" else 1, i, n)

            def negate_max(n, u):
                s = u % SLOTS
                act.wait_ge(s_mt, 8 * n + u + 1)
                act.activation(neg_max[:], turned_max, ACT.Copy, scale=-1.0).then_inc(s_neg, 1)
                act.wait_ge(s_neg, 8 * n + u + 1)
                act.dma_start(q_stack[96:97, s, :, :].rearrange("p j (i t) -> p (j i) t", i=NT).bitcast(FP32),
                              neg_max[:].bitcast(FP32)).then_inc(s_negrow[s], 16)

            def copy_values(b, u):
                act.wait_ge(s_pv, 8 * b + u + 1)
                act.activation(values[0:PV_ROWS, :], pv_bank[0:PV_ROWS, :], ACT.Copy).then_inc(s_pvcopy, 1)

            def exponentials(b, u, j, k):
                act.wait_ge(s_st, 48 * b + 6 * u + 3 * j + k + 1)
                act.activation(prob[j][:, UNIT_COL[k]:UNIT_COL[k] + UNIT_LEN[k]],
                               exp_bank[(3 * j + k) % 2][:, 0:UNIT_LEN[k]], ACT.Exp, scale=SCALE).then_inc(s_exp, 1)

            def first_hi(p):
                kind, i = FIRST_TURNS[p]
                act.wait_ge(s_turn, p + 1)
                act.activation((wt_hi if kind == "W" else xt_hi)[:, :, P * i:P * i + P],
                               first_bank(p)[:].rearrange("p (k c) -> p k c", k=NK), ACT.Copy).then_inc(s_thi, 1)

            def first_down(p):
                kind, i = FIRST_TURNS[p]
                if kind == "X" and i == 0:
                    act.wait_ge(s_xround, 1)
                else:
                    act.wait_ge(s_round, i + 1 if kind == "W" else NT + i)
                for j in range(NK):
                    if kind == "W":
                        part, down = tile_buf[:, i, P * j:P * j + P], w_down[:, NK * i + j:NK * i + j + 1]
                    else:
                        part, down = first_x[:, i, P * j:P * j + P], x_down[:, i, j:j + 1]
                    last = act.activation(part, part, ACT.Copy, scale=down)
                last.then_inc(s_quant, 1)

            def weight_hi(k):
                act.wait_ge(s_wscaled, k + 1)
                raw = raw_w[k]
                act.activation(w_hi[:, k, 0:2 * C].rearrange("p (h e) -> p h e", e=D)[:, :, 0:DS],
                               raw[:, 0:2 * H * DS].rearrange("p (h e) -> p h e", e=DS), ACT.Copy)
                act.activation(w_hi[:, k, 0:2 * C].rearrange("p (h e) -> p h e", e=D)[:, :, DS:D],
                               tails[k].rearrange("p q h e -> p (q h) e"), ACT.Copy)
                act.activation(w_hi[:, k, 2 * C:NF], raw[:, 2 * H * DS:2 * H * DS + C],
                               ACT.Copy).then_inc(s_whi, 1)

            for p in range(2 * NT):
                first_down(p)
                if 1 <= p <= NT:
                    first_hi(p - 1)
                if p >= NT:
                    first_hi(p)
            for k in range(NK):
                weight_hi(k)
            for p in range(2 * NT, 3 * NT):
                first_hi(p)
            act.wait_ge(s_wvlo, 1)
            qk_split_hi(0, 0, 0, first=True)
            qk_split_hi(1, 0, 0, first=True)
            act.wait_ge(s_wload[NK], 16)
            act.activation(wp_hi[:], raw_wp, ACT.Copy).then_inc(s_whi, 1)
            for i in range(3):
                side("V", i, 0)
            qk_split_hi(0, 1, 0, first=True)
            side("V", 3, 0)
            qk_split_hi(1, 1, 0, first=True)

            def body(b, more):
                def fill(u, gap):
                    for kind, i in pieces(u, gap, more):
                        if kind != "Y":
                            side(kind, i, b if kind in "VQK" else b + 1)

                def down(u, gap):
                    for k in DOWN.get((u, gap), []) if more else []:
                        scale_down(b + 1, k)

                def exp_pair(u, pair):
                    for unit in (2 * pair, 2 * pair + 1):
                        exponentials(b, u, unit // 3, unit % 3)

                def y_hi(i):
                    act.wait_ge(s_yt, NT * b + i + 1)
                    act.activation(wt_hi[:, :, P * i:P * i + P], y_bank[i][:].rearrange("p (k c) -> p k c", k=NK),
                                   ACT.Copy).then_inc(s_yhi, 1)

                def evacuate(u, gap):
                    down(u, gap)
                    fill(u, gap)

                for u in range(STEPS):
                    negate_max(b, u)
                    evacuate(u, 0)
                    if u:
                        copy_values(b, u - 1)
                    exp_pair(u, 0)
                    evacuate(u, 1)
                    exp_pair(u, 1)
                    evacuate(u, 2)
                    exp_pair(u, 2)
                    evacuate(u, 3)
                copy_values(b, STEPS - 1)
                if more:
                    side("V", 0, b + 1)
                    side("V", 1, b + 1)
                for i in range(3):
                    y_hi(i)
                if more:
                    side("V", 2, b + 1)
                    side("V", 3, b + 1)
                y_hi(3)
            per_batch(act, body)

        @block.vector
        def _(dve):
            chain = Chain(dve, s_dve)

            def x_tile(n, i):
                return x_all[:, n % 2, i, :] if isinstance(n, int) else x_all[:, bass.ds(n % 2, 1), i, :]

            def like_x(ap, n):
                return ap if isinstance(n, int) else ap.unsqueeze(1)

            def ctx_maximum(n, i):
                dve.wait_ge(s_ctxload[i], 16 * n + 16)
                last = dve.tensor_reduce(w_amax[:, NK * i:NK * i + NK],
                                         ctx_raw[:, i, :].rearrange("p (k c) -> p k c", k=NK),
                                         AX.X, ALU.max, apply_absolute_value=True)
                if i == NT - 1:
                    last.then_inc(s_amax, 1)

            def scales(amax, up, down, eps):
                chain(dve.tensor_scalar(down, amax, eps, None, ALU.max))
                chain(dve.reciprocal(up, down))
                dve.tensor_scalar(up, up, FP8_MAX, None, ALU.mult)
                return dve.tensor_scalar(down, down, 1.0 / FP8_MAX, None, ALU.mult)

            def ctx_scales(n):
                dve.wait_ge(s_top, n + 1)
                scales(w_top[:], w_up[:], w_down[:], W_EPS).then_inc(s_wscale, 1)

            def x_stat(n, i):
                wait_apart(dve, s_xload[i], 16 * n + 16)
                last = dve.bn_stats(bn1[:, i, :], x_tile(n, i))
                if i == NT - 1:
                    chain(last, wait_apart)
                    for t in range(NT):
                        last = dve.bn_aggr(mv1[:, t, :], bn1[:, t, :])
                    last.then_inc(s_var1, 1)

            def layernorm_x(n, i, first=False):
                if i == 0:
                    dve.wait_ge(s_rstd1, n + 1)
                if not first:
                    dve.wait_ge(s_turn, 12 * n + i + 1)
                buf = first_x[:, i, :] if first else tile_buf[:, i, :]
                chain(dve.tensor_scalar(like_x(buf, n), x_tile(n, i), mv1[:, i, 0:1], rstd1[:, i:i + 1],
                                        ALU.subtract, ALU.mult))
                chain(dve.tensor_reduce(x_amax[:, i, :], buf.rearrange("p (k c) -> p k c", k=NK),
                                        AX.X, ALU.max, apply_absolute_value=True))
                last = scales(x_amax[:, i, :], x_up[:, i, :], x_down[:, i, :], ACT_EPS)
                if first and i == 0:
                    chain(last)
                else:
                    last.then_inc(s_xscale, 1)

            def rounding(n, k):
                dve.wait_ge(s_scaled, 8 * n + k + 1)
                m = magic(n, k)
                chain(dve.tensor_scalar(m.bitcast(U16), tile_buf[:, k % 4, :].bitcast(U16)[:, 1::2],
                                        EXPONENT_BITS, None, ALU.bitwise_and))
                dve.tensor_scalar(m, m, MIN_NORMAL, MAGIC, ALU.max, ALU.mult).then_inc(s_magic, 1)

            def turned_lo(k, n):
                dve.wait_ge(s_thi, 12 * n + k + 1)
                hi, lo = (wt_hi, wt_lo) if k < NT else (xt_hi, xt_lo)
                cols = slice(P * (k % 4), P * (k % 4) + P)
                dve.tensor_tensor(lo[:, :, cols], turn_bank[:].rearrange("p (k c) -> p k c", k=NK),
                                  hi[:, :, cols].bitcast(FP32), ALU.subtract).then_inc(s_tlo, 1)

            def residual(n, i):
                dve.wait_ge(s_cross, NT * n + i + 1)
                chain(dve.scalar_tensor_tensor(x_tile(n, i), like_x(mm_bank[i % 2][:], n), gates[:, 0:1],
                                               x_tile(n, i), ALU.mult, ALU.add), wait_apart)
                chain(dve.bn_stats(bn2[:, i, :], x_tile(n, i)), wait_apart)
                dve.bn_aggr(mv2[:, i, :], bn2[:, i, :]).then_inc(s_x1, 1)

            def layernorm_x1(n, i):
                if i % 2 == 0:
                    dve.wait_ge(s_rstd2, 2 * n + i // 2 + 1)
                dve.wait_ge(s_turn, 12 * n + NT + i + 1)
                dve.tensor_scalar(like_x(tile_buf[:, i, :], n), x_tile(n, i), mv2[:, i, 0:1],
                                  rstd2[:, i:i + 1], ALU.subtract, ALU.mult).then_inc(s_hn, 1)

            def qk_split_lo(w, g, n):
                dve.wait_ge(s_qkhi, 8 * n + 2 * g + w + 1)
                dve.tensor_tensor(qk_lo[:, g % 2, w, :], mm_bank[w][:], qk_hi[:, g % 2, w, :].bitcast(FP32),
                                  ALU.subtract).then_inc(s_qklo, 1)

            def side(kind, i, n):
                if kind in "WXH":
                    turned_lo("WXH".index(kind) * NT + i, n)
                elif kind == "S":
                    residual(n, i)
                elif kind in "qkQK":
                    qk_split_lo(0 if kind in "qQ" else 1, i, n)

            def maxima(n, u, j, k):
                unit = 3 * j + k
                dve.wait_ge(s_sm, 48 * n + 6 * u + unit + 1)
                for i, col in MAX_UNITS[k]:
                    last = dve.tensor_reduce(row_max[:, u % 2, NT * j + i:NT * j + i + 1],
                                             max_bank[unit % 2][:, col:col + P * (i + 1)], AX.X, ALU.max)
                last.then_inc(s_max, 1)

            def normalise(b, u):
                dve.wait_ge(s_pvt, 8 * b + u + 1)
                pv = pv_bank[:].rearrange("p (i j e) -> p j i e", j=2, i=NT)
                rd = rden[:].rearrange("p (j i) -> p j i", j=2)
                chain(dve.reciprocal(rd, pv[:, :, :, D]))
                dve.tensor_tensor(y[:, :, 2 * D * u:2 * D * u + 2 * D].rearrange("p i (j d) -> p j i d", j=2),
                                  pv[:, :, :, 0:D], rd.unsqueeze(3).broadcast_to([P, 2, NT, D]),
                                  ALU.mult).then_inc(s_norm, 1)

            def first_magic(i):
                if i:
                    dve.wait_ge(s_scaled, NT + i)
                if i == 3:
                    dve.wait_ge(s_round, NT + 1)
                m = magic(0, NT + i)
                chain(dve.tensor_scalar(m.bitcast(U16), first_x[:, i, :].bitcast(U16)[:, 1::2],
                                        EXPONENT_BITS, None, ALU.bitwise_and))
                return dve.tensor_scalar(m, m, MIN_NORMAL, MAGIC, ALU.max, ALU.mult)

            def first_rounding(i):
                buf = first_x[:, i, :]
                blocks = buf.rearrange("p (k c) -> p k c", k=NK)
                chain(dve.tensor_tensor(blocks, blocks, x_up[:, i, :].unsqueeze(2).broadcast_to([P, NK, P]), ALU.mult))
                chain(first_magic(i))
                chain(dve.tensor_tensor(buf, buf, magic(0, NT + i), ALU.add))
                dve.tensor_tensor(buf, buf, magic(0, NT + i), ALU.subtract).then_inc(s_xround, 1)

            def first_lo(p):
                kind, i = FIRST_TURNS[p]
                dve.wait_ge(s_thi, p + 1)
                hi, lo = (wt_hi, wt_lo) if kind == "W" else (xt_hi, xt_lo)
                cols = slice(P * i, P * i + P)
                dve.tensor_tensor(lo[:, :, cols], first_bank(p)[:].rearrange("p (k c) -> p k c", k=NK),
                                  hi[:, :, cols].bitcast(FP32), ALU.subtract).then_inc(s_tlo, 1)

            def weight_chunk(k):
                raw, tail = raw_w[k], tails[k]
                dve.wait_ge(s_wload[k], 16)
                std = raw[:, 0:2 * H * DS].rearrange("p (q h e) -> p q h e", q=2, h=H)
                v0 = 2 * H * DS
                low = raw[:, v0 + C:NF].rearrange("p (q h e) -> p q h e", q=2, h=H)
                for q in range(2):
                    dve.tensor_tensor(std[:, q], std[:, q],
                                      wsr_root[:, 0, :].unsqueeze(2).broadcast_to([P, H, DS]), ALU.mult)
                    last = dve.tensor_tensor(low[:, q], low[:, q],
                                             wsr_root[:, 1, :].unsqueeze(2).broadcast_to([P, H, R]), ALU.mult)
                chain(last)
                chain(dve.tensor_copy(tail, low))
                dve.copy_predicated(tail[:, 0], swap, low[:, 1])
                dve.copy_predicated(tail[:, 1], swap, low[:, 0]).then_inc(s_wscaled, 1)

            dve.memset(pv_bank[:], 0.0).then_inc(s_cleared, 1)
            for i in range(NT):
                x_stat(0, i)
            for i in range(NT):
                ctx_maximum(0, i)
            ctx_scales(0)
            layernorm_x(0, 0, first=True)
            rounding(0, 0)
            rounding(0, 1)
            dve.wait_ge(s_root, 1)
            dve.wait_ge(s_const, 1)
            dve.tensor_scalar(root_diag, ident[0:2 * H, 0:2 * H], root_col[:, 0:1], None,
                              ALU.mult).then_inc(s_diag, 1)
            first_rounding(0)
            layernorm_x(0, 1, first=True)
            rounding(0, 2)
            rounding(0, 3)
            first_lo(0)
            first_lo(1)
            layernorm_x(0, 2, first=True)
            first_lo(2)
            first_magic(1).then_inc(s_magic, 1)
            first_lo(3)
            layernorm_x(0, 3, first=True)
            first_magic(2).then_inc(s_magic, 1)
            first_lo(4)
            chain(dve.tensor_scalar(swap, wsr[:, 1, :].unsqueeze(2).broadcast_to([P, H, R]), 0.1, None,
                                    ALU.is_gt))
            dve.wait_ge(s_spread, 1)
            chain(dve.tensor_copy(wsr_root[:].rearrange("p q h -> p (q h)"), exp_bank[1][:, 0:2 * H]))
            first_magic(3).then_inc(s_magic, 1)
            first_lo(5)
            weight_chunk(0)
            weight_chunk(1)
            weight_chunk(2)
            first_lo(6)
            dve.wait_ge(s_tanh, 1)
            residual(0, 0)
            first_lo(7)
            residual(0, 1)
            weight_chunk(3)
            residual(0, 2)
            residual(0, 3)
            layernorm_x1(0, 0)
            layernorm_x1(0, 1)
            layernorm_x1(0, 2)
            layernorm_x1(0, 3)
            first_lo(8)
            first_lo(9)
            first_lo(10)
            first_lo(11)
            qk_split_lo(0, 0, 0)
            qk_split_lo(1, 0, 0)
            maxima(0, 0, 0, 0)
            maxima(0, 0, 0, 1)
            qk_split_lo(0, 1, 0)
            maxima(0, 0, 0, 2)
            maxima(0, 0, 1, 0)
            maxima(0, 0, 1, 1)
            maxima(0, 0, 1, 2)
            qk_split_lo(1, 1, 0)
            dve.sem_inc(s_magic, 1)
            dve.sem_inc(s_xscale, 1)
            first = chain.n
            dve.sem_inc(s_outt, FIRST_OUT)

            own = {(0, -1): [(ctx_maximum, [0]), (ctx_maximum, [1]), (ctx_maximum, [2]), (ctx_maximum, [3])],
                   (0, 0): [(ctx_scales, [])],
                   (0, 1): [(x_stat, [0]), (x_stat, [1])],
                   (0, 2): [(rounding, [0]), (x_stat, [2])],
                   (0, 3): [(x_stat, [3]), (rounding, [1])],
                   (1, 0): [(rounding, [2])],
                   (1, 1): [(rounding, [3])],
                   (1, 2): [(layernorm_x, [0])],
                   (2, -1): [(layernorm_x, [1])],
                   (2, 0): [(rounding, [4])],
                   (2, 2): [(rounding, [5]), (layernorm_x, [2])],
                   (2, 3): [(layernorm_x, [3])],
                   (3, 0): [(rounding, [6])],
                   (3, 1): [(rounding, [7])],
                   (5, -1): [(layernorm_x1, [0]), (layernorm_x1, [1])],
                   (5, 1): [(layernorm_x1, [2]), (layernorm_x1, [3])]}

            def body(b, more):
                n = b + 1
                chain.at(first + DVE_CHAIN * b)

                def fill(u, gap):
                    for kind, i in pieces(u, gap, more):
                        if kind != "Y":
                            side(kind, i, b if kind in "VQK" else n)
                        elif i % 2:
                            output(B - 2, i // 2)

                def output(b, i):
                    dve.wait_ge(s_wpmm, NT * b + i + 1)
                    dve.scalar_tensor_tensor(x_tile(b, i), like_x(mm_bank[i % 2][:], b), gates[:, 1:2],
                                             x_tile(b, i), ALU.mult, ALU.add).then_inc(s_outt, 1)

                def beside(u, gap):
                    for f, a in own.get((u, gap), []) if more else []:
                        f(n, *a)

                def max_pair(n, u, pair):
                    for unit in (2 * pair, 2 * pair + 1):
                        maxima(n, u, unit // 3, unit % 3)

                for u in range(STEPS):
                    if u + 1 < STEPS:
                        max_pair(b, u + 1, 0)
                    beside(u, -1)
                    fill(u, 0)
                    beside(u, 0)
                    if u + 1 < STEPS:
                        max_pair(b, u + 1, 1)
                    fill(u, 1)
                    beside(u, 1)
                    if u:
                        normalise(b, u - 1)
                    if u + 1 < STEPS:
                        max_pair(b, u + 1, 2)
                    for gap in (2, 3):
                        fill(u, gap)
                        beside(u, gap)
                normalise(b, STEPS - 1)

                def y_lo(i):
                    dve.wait_ge(s_yhi, NT * b + i + 1)
                    dve.tensor_tensor(wt_lo[:, :, P * i:P * i + P], y_bank[i][:].rearrange("p (k c) -> p k c", k=NK),
                                      wt_hi[:, :, P * i:P * i + P].bitcast(FP32), ALU.subtract).then_inc(s_ylo, 1)

                for i in range(3):
                    y_lo(i)
                if more:
                    for pair in range(3):
                        max_pair(n, 0, pair)
                y_lo(3)
                if not late_output(b):
                    for i in range(NT):
                        output(b, i)
                if more:
                    assert chain.n == DVE_CHAIN, chain.n

            per_batch(dve, body, peeled=2)


_INS = ["x", "ctx_2048", "g_xattn", "g_ffn", "L0_ffn_Wa", "L0_ffn_Wp", "L0_ffn_w_std", "L0_ffn_w_rec"]


def kernel(**inputs):
    import numpy as np
    import concourse.bacc as bacc
    from concourse.bass_utils import run_bass_kernel_spmd

    nc = bacc.Bacc("TRN2", target_bir_lowering=False, num_devices=1)
    arrays, args = {}, []
    for name in _INS:
        a = np.ascontiguousarray(inputs[name])
        arrays[f"in_{name}"] = a
        args.append(nc.dram_tensor(f"in_{name}", a.shape, mybir.dt.from_np(a.dtype), kind="ExternalInput").ap())
    out = nc.dram_tensor("out", (B, T, C), FP32, kind="ExternalOutput").ap()
    flamingo_block(nc, *args, out)
    r = run_bass_kernel_spmd(nc, [arrays], core_ids=[0])
    return r.results[0]["out"]
```
